# Optimizing a Trainium2 kernel written in Bass

```python
import numpy as np
import jax
import jax.numpy as jnp

def _softmax(x, axis=-1):
    return jax.nn.softmax(x, axis=axis)

def _gelu(x):
    return jax.nn.gelu(x, approximate=True)

def _silu(x):
    return jax.nn.silu(x)

def _sigmoid(x):
    return jax.nn.sigmoid(x)

def _layernorm(x, axis=-1, eps=1e-05):
    m = jnp.mean(x, axis=axis, keepdims=True)
    v = jnp.var(x, axis=axis, keepdims=True)
    return (x - m) / jnp.sqrt(v + eps)

def _scatter_add(tgt, idx, src, axis=0):
    return tgt.at[idx].add(src)

def _segment_sum(src, seg, n):
    return jax.ops.segment_sum(src, seg, n)
kernel_name = 'mk_xattn_ffn_d4_seqx_r8_a59b2f'

def setup_inputs(seed: int=0):
    np.random.seed(seed)
    _w = jnp.asarray

    def _rec_inputs():
        import jax
        import jax.numpy as jnp
        _rk = jax.random.key(seed)
        x = -0.0005207 + 1.001 * jax.random.normal(jax.random.fold_in(_rk, 1), (32, 128, 128), jnp.float32)
        _lenS = 128 - jax.random.randint(jax.random.fold_in(_rk, 7), (32,), 0, max(1, 128 // 4) + 1, jnp.int32)
        _lenS2 = 128 - jax.random.randint(jax.random.fold_in(_rk, 8), (32,), 0, max(1, 128 // 4) + 1, jnp.int32)
        _ctx_1024P = jax.random.normal(jax.random.fold_in(_rk, 11), (32, 16, 128), jnp.float32)
        _ctx_1024c = jax.random.dirichlet(jax.random.fold_in(_rk, 511), 0.3 * jnp.ones((16,), jnp.float32), (32, 128))
        _ctx_1024t = jnp.einsum('bsk,bkd->bsd', _ctx_1024c, _ctx_1024P)
        _ctx_1024t = _ctx_1024t * jax.lax.rsqrt(jnp.mean(jnp.square(_ctx_1024t)) + 1e-12) * 0.953939
        ctx_1024 = -0.000514642 + 1.00011 * (_ctx_1024t + 0.3 * jax.random.normal(jax.random.fold_in(_rk, 611), (32, 128, 128), jnp.float32))
        return (x, ctx_1024)
    x, ctx_1024 = _rec_inputs()

    def _L0_xattn_setup():
        import jax, jax.numpy as jnp
        import numpy as np
        D_MODEL = 128
        FFN = 512
        E = 8
        K = 2
        B, S = (4, 64)
        key = jax.random.key(seed)
        ks = jax.random.split(key, 8)
        scale_in = 1.0 / np.sqrt(D_MODEL)
        scale_ffn = 1.0 / np.sqrt(FFN)
        return {'x': jax.random.normal(ks[0], (B, S, D_MODEL), jnp.float32), 'context': jax.random.normal(ks[1], (B, S, D_MODEL), jnp.float32), 'Wg': jax.random.normal(ks[2], (D_MODEL, E), jnp.float32) * scale_in, 'bg': jnp.zeros((E,), jnp.float32), 'W1': jax.random.normal(ks[3], (E, D_MODEL, FFN), jnp.float32) * scale_in, 'b1': jnp.zeros((E, FFN), jnp.float32), 'W2': jax.random.normal(ks[4], (E, FFN, D_MODEL), jnp.float32) * scale_ffn, 'b2': jnp.zeros((E, D_MODEL), jnp.float32)}
    _L0_xattn_all = _L0_xattn_setup()
    _L0_xattn_in = {k: v for k, v in _L0_xattn_all.items() if k in ('Wg', 'bg', 'W1', 'b1', 'W2', 'b2')}
    del _L0_xattn_all

    def _L0_ffn_setup():
        import jax, jax.numpy as jnp
        import numpy as np
        D = 128
        F = 4 * D
        E = 8
        NS = 2
        TOP_K = 2
        B, S = (2, 128)
        key = jax.random.key(seed)
        ks = jax.random.split(key, 7)
        w = 1.0 / np.sqrt(D)
        wf = 1.0 / np.sqrt(F)
        return {'x': jax.random.normal(ks[0], (B, S, D), jnp.float32), 'centroids': jax.random.normal(ks[1], (E, D), jnp.float32) * w, 'routing_bias': jnp.zeros((E,), jnp.float32), 'Wfc_r': jax.random.normal(ks[2], (E, F, D), jnp.float32) * w, 'Wproj_r': jax.random.normal(ks[3], (E, D, F), jnp.float32) * wf, 'Wfc_sh': jax.random.normal(ks[4], (NS, F, D), jnp.float32) * w, 'Wproj_sh': jax.random.normal(ks[5], (NS, D, F), jnp.float32) * wf}
    _L0_ffn_all = _L0_ffn_setup()
    _L0_ffn_in = {k: v for k, v in _L0_ffn_all.items() if k in ('centroids', 'routing_bias', 'Wfc_r', 'Wproj_r', 'Wfc_sh', 'Wproj_sh')}
    del _L0_ffn_all

    def _L1_xattn_setup():
        import jax, jax.numpy as jnp
        import numpy as np
        B, SQ, SKV, E, H = (4, 256, 256, 128, 16)
        HD = E // H

        def stablemax(x):
            s = jnp.where(x >= 0, x + 1.0, 1.0 / (1.0 - x))
            return s / jnp.sum(s, axis=-1, keepdims=True)
        key = jax.random.key(seed)
        ks = jax.random.split(key, 6)
        scale = 1.0 / np.sqrt(E)
        return {'query': jax.random.normal(ks[0], (B, SQ, E), jnp.float32), 'key_value': jax.random.normal(ks[1], (B, SKV, E), jnp.float32), 'Wq': jax.random.normal(ks[2], (E, E), jnp.float32) * scale, 'bq': jnp.zeros((E,), jnp.float32), 'Wk': jax.random.normal(ks[3], (E, E), jnp.float32) * scale, 'bk': jnp.zeros((E,), jnp.float32), 'Wv': jax.random.normal(ks[4], (E, E), jnp.float32) * scale, 'bv': jnp.zeros((E,), jnp.float32), 'Wo': jax.random.normal(ks[5], (E, E), jnp.float32) * scale, 'bo': jnp.zeros((E,), jnp.float32)}
    _L1_xattn_all = _L1_xattn_setup()
    _L1_xattn_in = {k: v for k, v in _L1_xattn_all.items() if k in ('Wq', 'bq', 'Wk', 'bk', 'Wv', 'bv', 'Wo', 'bo')}
    del _L1_xattn_all

    def _L1_ffn_setup():
        import jax, jax.numpy as jnp
        import numpy as np
        E = 8
        K = 2
        D = 128
        H = 512
        CAP_FACTOR = 1.0
        key = jax.random.key(seed)
        ks = jax.random.split(key, 5)
        x = jax.random.normal(ks[0], (4, 256, D), jnp.float32)
        gate_w = jax.random.normal(ks[1], (E, D), jnp.float32) * 0.02
        fc1_w = jax.random.normal(ks[2], (E, H, D), jnp.float32) * 0.02
        fc1_b = jnp.zeros((E, 1, H), jnp.float32)
        fc2_w = jax.random.normal(ks[3], (E, H, D), jnp.float32) * 0.02
        fc2_b = jnp.zeros((E, 1, D), jnp.float32)
        return {'x': x, 'gate_w': gate_w, 'fc1_w': fc1_w, 'fc1_b': fc1_b, 'fc2_w': fc2_w, 'fc2_b': fc2_b}
    _L1_ffn_all = _L1_ffn_setup()
    _L1_ffn_in = {k: v for k, v in _L1_ffn_all.items() if k in ('gate_w', 'fc1_w', 'fc1_b', 'fc2_w', 'fc2_b')}
    del _L1_ffn_all

    def _L2_xattn_setup():
        import jax, jax.numpy as jnp
        import numpy as np
        import math
        NUM_HEAD = 16
        D_MODEL = 128
        BATCH = 2
        SEQ = 256

        def _split_heads(x):
            B, S, D = x.shape
            return x.reshape(B, S, NUM_HEAD, D // NUM_HEAD).transpose(0, 2, 1, 3)
        key = jax.random.key(seed)
        k1, k2, k3, k4 = jax.random.split(key, 4)
        scale = 1.0 / math.sqrt(D_MODEL)
        return {'query': jax.random.normal(k1, (BATCH, SEQ, D_MODEL), dtype=jnp.float32), 'key': jax.random.normal(k2, (BATCH, SEQ, D_MODEL), dtype=jnp.float32), 'value': jax.random.normal(k3, (BATCH, SEQ, D_MODEL), dtype=jnp.float32), 'w_concat': jax.random.normal(k4, (D_MODEL, D_MODEL), dtype=jnp.float32) * scale}
    _L2_xattn_all = _L2_xattn_setup()
    _L2_xattn_in = {k: v for k, v in _L2_xattn_all.items() if k in ('w_concat',)}
    del _L2_xattn_all

    def _L2_ffn_setup():
        import jax, jax.numpy as jnp
        import numpy as np
        FP8_MAX = 448.0
        SCALE = 1.0
        _FP8_DTYPE = getattr(jnp, 'float8_e4m3fn', jnp.float16)

        def quantize_e4m3(t, scale):
            return jnp.clip(t / scale, -FP8_MAX, FP8_MAX).astype(_FP8_DTYPE)
        key = jax.random.key(seed)
        kx, kw = jax.random.split(key)
        B, N, C, F = (8, 512, 128, 128)
        x = jax.random.normal(kx, (B, N, C), dtype=jnp.float32)
        weight = jax.random.normal(kw, (F, C), dtype=jnp.float32) * 0.02
        bias = jnp.zeros((F,), dtype=jnp.float32)
        return {'x': x, 'weight': weight, 'bias': bias}
    _L2_ffn_all = _L2_ffn_setup()
    _L2_ffn_in = {k: v for k, v in _L2_ffn_all.items() if k in ('weight', 'bias')}
    del _L2_ffn_all

    def _L3_xattn_setup():
        import jax, jax.numpy as jnp
        import numpy as np
        B, S, D, H = (4, 256, 128, 16)
        DK = D // H
        key = jax.random.key(seed)
        ks = jax.random.split(key, 7)
        scale = 0.02
        query = jax.random.normal(ks[0], (B, S, D), dtype=jnp.float32)
        k_in = jax.random.normal(ks[1], (B, S, D), dtype=jnp.float32)
        v_in = jax.random.normal(ks[2], (B, S, D), dtype=jnp.float32)
        Wq = jax.random.normal(ks[3], (H, D, DK), dtype=jnp.float32) * scale
        Wk = jax.random.normal(ks[4], (H, D, DK), dtype=jnp.float32) * scale
        Wv = jax.random.normal(ks[5], (H, D, DK), dtype=jnp.float32) * scale
        Wo = jax.random.normal(ks[6], (D, D), dtype=jnp.float32) * scale
        return {'query': query, 'key': k_in, 'value': v_in, 'Wq': Wq, 'Wk': Wk, 'Wv': Wv, 'Wo': Wo}
    _L3_xattn_all = _L3_xattn_setup()
    _L3_xattn_in = {k: v for k, v in _L3_xattn_all.items() if k in ('Wq', 'Wk', 'Wv', 'Wo')}
    del _L3_xattn_all

    def _L3_ffn_setup():
        import jax, jax.numpy as jnp
        import numpy as np
        TOPK = 4
        key = jax.random.key(seed)
        ks = jax.random.split(key, 9)
        B, T, D = (4, 256, 128)
        E, H = (32, 128)
        HS = H * TOPK
        s = lambda k, shape, fan: jax.random.normal(k, shape, dtype=jnp.float32) / np.sqrt(fan)
        return {'x': jax.random.normal(ks[0], (B, T, D), dtype=jnp.float32), 'router_w': s(ks[1], (E, D), D), 'router_bias': jnp.zeros((E,), dtype=jnp.float32), 'gate_w': s(ks[2], (E, H, D), D), 'up_w': s(ks[3], (E, H, D), D), 'down_w': s(ks[4], (E, D, H), H), 'sgate_w': s(ks[5], (HS, D), D), 'sup_w': s(ks[6], (HS, D), D), 'sdown_w': s(ks[7], (D, HS), HS)}
    _L3_ffn_all = _L3_ffn_setup()
    _L3_ffn_in = {k: v for k, v in _L3_ffn_all.items() if k in ('router_w', 'router_bias', 'gate_w', 'up_w', 'down_w', 'sgate_w', 'sup_w', 'sdown_w')}
    del _L3_ffn_all
    return {'x': x, 'ctx_1024': ctx_1024, 'L0_xattn_Wg': _L0_xattn_in['Wg'], 'L0_xattn_bg': _L0_xattn_in['bg'], 'L0_xattn_W1': _L0_xattn_in['W1'], 'L0_xattn_b1': _L0_xattn_in['b1'], 'L0_xattn_W2': _L0_xattn_in['W2'], 'L0_xattn_b2': _L0_xattn_in['b2'], 'L0_ffn_centroids': _L0_ffn_in['centroids'], 'L0_ffn_routing_bias': _L0_ffn_in['routing_bias'], 'L0_ffn_Wfc_r': _L0_ffn_in['Wfc_r'], 'L0_ffn_Wproj_r': _L0_ffn_in['Wproj_r'], 'L0_ffn_Wfc_sh': _L0_ffn_in['Wfc_sh'], 'L0_ffn_Wproj_sh': _L0_ffn_in['Wproj_sh'], 'L1_xattn_Wq': _L1_xattn_in['Wq'], 'L1_xattn_bq': _L1_xattn_in['bq'], 'L1_xattn_Wk': _L1_xattn_in['Wk'], 'L1_xattn_bk': _L1_xattn_in['bk'], 'L1_xattn_Wv': _L1_xattn_in['Wv'], 'L1_xattn_bv': _L1_xattn_in['bv'], 'L1_xattn_Wo': _L1_xattn_in['Wo'], 'L1_xattn_bo': _L1_xattn_in['bo'], 'L1_ffn_gate_w': _L1_ffn_in['gate_w'], 'L1_ffn_fc1_w': _L1_ffn_in['fc1_w'], 'L1_ffn_fc1_b': _L1_ffn_in['fc1_b'], 'L1_ffn_fc2_w': _L1_ffn_in['fc2_w'], 'L1_ffn_fc2_b': _L1_ffn_in['fc2_b'], 'L2_xattn_w_concat': _L2_xattn_in['w_concat'], 'L2_ffn_weight': _L2_ffn_in['weight'], 'L2_ffn_bias': _L2_ffn_in['bias'], 'L3_xattn_Wq': _L3_xattn_in['Wq'], 'L3_xattn_Wk': _L3_xattn_in['Wk'], 'L3_xattn_Wv': _L3_xattn_in['Wv'], 'L3_xattn_Wo': _L3_xattn_in['Wo'], 'L3_ffn_router_w': _L3_ffn_in['router_w'], 'L3_ffn_router_bias': _L3_ffn_in['router_bias'], 'L3_ffn_gate_w': _L3_ffn_in['gate_w'], 'L3_ffn_up_w': _L3_ffn_in['up_w'], 'L3_ffn_down_w': _L3_ffn_in['down_w'], 'L3_ffn_sgate_w': _L3_ffn_in['sgate_w'], 'L3_ffn_sup_w': _L3_ffn_in['sup_w'], 'L3_ffn_sdown_w': _L3_ffn_in['sdown_w']}

def reference(x, ctx_1024, L0_xattn_Wg, L0_xattn_bg, L0_xattn_W1, L0_xattn_b1, L0_xattn_W2, L0_xattn_b2, L0_ffn_centroids, L0_ffn_routing_bias, L0_ffn_Wfc_r, L0_ffn_Wproj_r, L0_ffn_Wfc_sh, L0_ffn_Wproj_sh, L1_xattn_Wq, L1_xattn_bq, L1_xattn_Wk, L1_xattn_bk, L1_xattn_Wv, L1_xattn_bv, L1_xattn_Wo, L1_xattn_bo, L1_ffn_gate_w, L1_ffn_fc1_w, L1_ffn_fc1_b, L1_ffn_fc2_w, L1_ffn_fc2_b, L2_xattn_w_concat, L2_ffn_weight, L2_ffn_bias, L3_xattn_Wq, L3_xattn_Wk, L3_xattn_Wv, L3_xattn_Wo, L3_ffn_router_w, L3_ffn_router_bias, L3_ffn_gate_w, L3_ffn_up_w, L3_ffn_down_w, L3_ffn_sgate_w, L3_ffn_sup_w, L3_ffn_sdown_w):
    import jax
    import jax.numpy as jnp

    def _L0_xattn_ref(x, context, Wg, bg, W1, b1, W2, b2):
        import jax, jax.numpy as jnp
        import numpy as np
        D_MODEL = 128
        FFN = 512
        E = 8
        K = 2
        B, S = (4, 64)
        logits = jnp.einsum('bsd,de->bse', context, Wg) + bg
        scores_topk, idx_topk = jax.lax.top_k(logits, K)
        weights = jax.nn.softmax(scores_topk, axis=-1)
        combine = jnp.sum(jax.nn.one_hot(idx_topk, E, dtype=weights.dtype) * weights[..., None], axis=-2)
        h = jax.nn.relu(jnp.einsum('bsd,edf->bsef', x, W1) + b1)
        y = jnp.einsum('bsef,efd->bsed', h, W2) + b2
        out = jnp.einsum('bsed,bse->bsd', y, combine)
        return out

    def _L0_ffn_ref(x, centroids, routing_bias, Wfc_r, Wproj_r, Wfc_sh, Wproj_sh):
        import jax, jax.numpy as jnp
        import numpy as np
        D = 128
        F = 4 * D
        E = 8
        NS = 2
        TOP_K = 2
        B, S = (2, 128)
        raw = jnp.einsum('bsd,ed->bse', x, centroids)
        routing_scores = jax.nn.sigmoid(raw)
        balanced = jax.nn.sigmoid(raw + routing_bias)
        _, top_idx = jax.lax.top_k(balanced, TOP_K)
        gathered = jnp.take_along_axis(routing_scores, top_idx, axis=-1)
        top_w = jax.nn.softmax(gathered, axis=-1)
        combine = jnp.sum(jax.nn.one_hot(top_idx, E, dtype=x.dtype) * top_w[..., None], axis=-2)
        h_sh = jax.nn.gelu(jnp.einsum('bsd,nfd->bsnf', x, Wfc_sh), approximate=False)
        shared_out = jnp.einsum('bsnf,ndf->bsd', h_sh, Wproj_sh)
        h_r = jax.nn.gelu(jnp.einsum('bsd,efd->bsef', x, Wfc_r), approximate=False)
        expert_out = jnp.einsum('bsef,edf->bsed', h_r, Wproj_r)
        routed_out = jnp.einsum('bsed,bse->bsd', expert_out, combine)
        return x + shared_out + routed_out

    def _L1_xattn_ref(query, key_value, Wq, bq, Wk, bk, Wv, bv, Wo, bo):
        import jax, jax.numpy as jnp
        import numpy as np
        B, SQ, SKV, E, H = (4, 256, 256, 128, 16)
        HD = E // H

        def stablemax(x):
            s = jnp.where(x >= 0, x + 1.0, 1.0 / (1.0 - x))
            return s / jnp.sum(s, axis=-1, keepdims=True)
        b = query.shape[0]
        q = query @ Wq.T + bq
        k = key_value @ Wk.T + bk
        v = key_value @ Wv.T + bv
        q = q.reshape(b, -1, H, HD).transpose(0, 2, 1, 3)
        k = k.reshape(b, -1, H, HD).transpose(0, 2, 1, 3)
        v = v.reshape(b, -1, H, HD).transpose(0, 2, 1, 3)
        scores = jnp.einsum('bhqd,bhkd->bhqk', q, k) / np.sqrt(HD).astype(np.float32)
        attn = stablemax(scores)
        context = jnp.einsum('bhqk,bhkd->bhqd', attn, v)
        context = context.transpose(0, 2, 1, 3).reshape(b, -1, E)
        return context @ Wo.T + bo

    def _L1_ffn_ref(x, gate_w, fc1_w, fc1_b, fc2_w, fc2_b):
        import jax, jax.numpy as jnp
        import numpy as np
        E = 8
        K = 2
        D = 128
        H = 512
        CAP_FACTOR = 1.0
        B, S, Dm = x.shape
        xf = x.reshape(-1, Dm)
        N = xf.shape[0]
        cap = int(K * CAP_FACTOR * ((N + E - 1) // E))
        logits = xf @ gate_w.T
        scores = jax.nn.softmax(logits, axis=-1)
        topv, topi = jax.lax.top_k(scores, K)
        gates = topv / jnp.sum(topv, axis=-1, keepdims=True)
        offset = jnp.zeros((E,), jnp.int32)
        locs = []
        for j in range(K):
            mask = jax.nn.one_hot(topi[:, j], E, dtype=jnp.int32)
            loc_in = jnp.cumsum(mask, axis=0) - 1 + offset[None, :]
            locs.append(jnp.take_along_axis(loc_in, topi[:, j:j + 1], axis=1)[:, 0])
            offset = offset + mask.sum(axis=0)
        loc = jnp.stack(locs, axis=1)
        valid = loc < cap
        flat_idx = jnp.where(valid, topi * cap + loc, 0)
        w = valid.astype(xf.dtype)
        disp = jnp.zeros((E * cap, Dm), xf.dtype)
        disp = disp.at[flat_idx.reshape(-1)].add((xf[:, None, :] * w[:, :, None]).reshape(-1, Dm))
        de = disp.reshape(E, cap, Dm)
        h = jax.nn.relu(jnp.einsum('ecd,ehd->ech', de, fc1_w) + fc1_b)
        eo = jnp.einsum('ech,ehd->ecd', h, fc2_w) + fc2_b
        gathered = eo.reshape(E * cap, Dm)[flat_idx]
        out = jnp.sum(gathered * (gates * w)[:, :, None], axis=1)
        return out.reshape(B, S, Dm)

    def _L2_xattn_ref(query, key, value, w_concat):
        import jax, jax.numpy as jnp
        import numpy as np
        import math
        NUM_HEAD = 16
        D_MODEL = 128
        BATCH = 2
        SEQ = 256

        def _split_heads(x):
            B, S, D = x.shape
            return x.reshape(B, S, NUM_HEAD, D // NUM_HEAD).transpose(0, 2, 1, 3)
        q = _split_heads(query)
        k = _split_heads(key)
        v = _split_heads(value)
        d_k = q.shape[-1]
        scores = jnp.einsum('bhqd,bhkd->bhqk', q, k) / math.sqrt(d_k)
        attn = jax.nn.softmax(scores, axis=-1)
        ctx = jnp.einsum('bhqk,bhkd->bhqd', attn, v)
        B, H, S, dk = ctx.shape
        x = ctx.transpose(0, 2, 1, 3).reshape(B, S, H * dk)
        return x @ w_concat.T

    def _L2_ffn_ref(x, weight, bias):
        import jax, jax.numpy as jnp
        import numpy as np
        FP8_MAX = 448.0
        SCALE = 1.0
        _FP8_DTYPE = getattr(jnp, 'float8_e4m3fn', jnp.float16)

        def quantize_e4m3(t, scale):
            return jnp.clip(t / scale, -FP8_MAX, FP8_MAX).astype(_FP8_DTYPE)
        B, N, C = x.shape
        x2d = x.reshape(B * N, C)
        x_mat = quantize_e4m3(x2d, SCALE).astype(jnp.float16)
        w_mat = quantize_e4m3(weight, SCALE).astype(jnp.float16)
        out2d = (x_mat @ w_mat.T).astype(jnp.float32) * (SCALE * SCALE)
        out2d = out2d + bias
        return out2d.reshape(B, N, -1)

    def _L3_xattn_ref(query, key, value, Wq, Wk, Wv, Wo):
        import jax, jax.numpy as jnp
        import numpy as np
        B, S, D, H = (4, 256, 128, 16)
        DK = D // H
        dk = Wq.shape[-1]
        q = jnp.einsum('bsd,hdk->bhsk', query, Wq)
        k = jnp.einsum('btd,hdk->bhtk', key, Wk)
        v = jnp.einsum('btd,hdk->bhtk', value, Wv)
        logits = jnp.einsum('bhsk,bhtk->bhst', q, k) / jnp.sqrt(jnp.float32(dk))
        attn = jax.nn.softmax(logits, axis=-1)
        ctx = jnp.einsum('bhst,bhtk->bhsk', attn, v)
        b, h, s, _ = ctx.shape
        concat = ctx.transpose(0, 2, 1, 3).reshape(b, s, h * dk)
        return jnp.einsum('bsd,ed->bse', concat, Wo)

    def _L3_ffn_ref(x, router_w, router_bias, gate_w, up_w, down_w, sgate_w, sup_w, sdown_w):
        import jax, jax.numpy as jnp
        import numpy as np
        TOPK = 4
        B, T, D = x.shape
        flat = x.reshape(B * T, D)
        logits = flat.astype(jnp.float32) @ router_w.T + router_bias
        scores = jax.nn.softmax(logits, axis=-1)
        topk_scores, topk_idx = jax.lax.top_k(scores, TOPK)
        topk_scores = topk_scores / jnp.clip(topk_scores.sum(axis=-1, keepdims=True), 1e-12, None)
        h = jax.nn.silu(jnp.einsum('nd,ehd->neh', flat, gate_w)) * jnp.einsum('nd,ehd->neh', flat, up_w)
        expert_out = jnp.einsum('neh,edh->ned', h, down_w)
        sel = jnp.take_along_axis(expert_out, topk_idx[:, :, None], axis=1)
        out = (sel * topk_scores.astype(flat.dtype)[:, :, None]).sum(axis=1)
        out = out + jax.nn.silu(flat @ sgate_w.T) * (flat @ sup_w.T) @ sdown_w.T
        return out.reshape(B, T, D)
    x = x + _L0_xattn_ref(_layernorm(x, axis=-1), ctx_1024, L0_xattn_Wg, L0_xattn_bg, L0_xattn_W1, L0_xattn_b1, L0_xattn_W2, L0_xattn_b2)
    x = x + _L0_ffn_ref(_layernorm(x, axis=-1), L0_ffn_centroids, L0_ffn_routing_bias, L0_ffn_Wfc_r, L0_ffn_Wproj_r, L0_ffn_Wfc_sh, L0_ffn_Wproj_sh)
    x = x + _L1_xattn_ref(_layernorm(x, axis=-1), ctx_1024, L1_xattn_Wq, L1_xattn_bq, L1_xattn_Wk, L1_xattn_bk, L1_xattn_Wv, L1_xattn_bv, L1_xattn_Wo, L1_xattn_bo)
    x = x + _L1_ffn_ref(_layernorm(x, axis=-1), L1_ffn_gate_w, L1_ffn_fc1_w, L1_ffn_fc1_b, L1_ffn_fc2_w, L1_ffn_fc2_b)
    x = x + _L2_xattn_ref(_layernorm(x, axis=-1), ctx_1024, ctx_1024, L2_xattn_w_concat)
    x = x + _L2_ffn_ref(_layernorm(x, axis=-1), L2_ffn_weight, L2_ffn_bias)
    x = x + _L3_xattn_ref(_layernorm(x, axis=-1), ctx_1024, ctx_1024, L3_xattn_Wq, L3_xattn_Wk, L3_xattn_Wv, L3_xattn_Wo)
    x = x + _L3_ffn_ref(_layernorm(x, axis=-1), L3_ffn_router_w, L3_ffn_router_bias, L3_ffn_gate_w, L3_ffn_up_w, L3_ffn_down_w, L3_ffn_sgate_w, L3_ffn_sup_w, L3_ffn_sdown_w)
    return x

_drawn_inputs = setup_inputs


def setup_inputs(seed=0):
    import zlib

    import numpy as np

    out = dict(_drawn_inputs(seed))
    spreads = {'L0_xattn_bg': (0.0, 0.1),
     'L0_xattn_b1': (0.0, 0.1),
     'L0_xattn_b2': (0.0, 0.1),
     'L0_ffn_routing_bias': (0.0, 0.1),
     'L1_xattn_bq': (0.0, 0.8),
     'L1_xattn_bk': (0.0, 2.0),
     'L1_xattn_bv': (0.0, 0.1),
     'L1_xattn_bo': (0.0, 0.1),
     'L1_ffn_fc1_b': (0.0, 0.613),
     'L1_ffn_fc2_b': (0.0, 0.1),
     'L2_ffn_bias': (0.0, 0.1),
     'L3_ffn_router_bias': (0.0, 0.1)}
    factors = {'L1_ffn_fc1_w': 2.698,
     'L3_xattn_Wq': 8.0,
     'L3_xattn_Wk': 8.0,
     'L3_xattn_Wv': 4.109,
     'L3_xattn_Wo': 4.098}
    for name, (base, spread) in spreads.items():
        noise = np.random.default_rng([zlib.crc32(name.encode()), seed]).standard_normal(out[name].shape)
        drawn = base * np.exp(spread * noise) if base else spread * noise
        out[name] = jnp.asarray(drawn.astype(out[name].dtype))
    for name, factor in factors.items():
        out[name] = (out[name] * factor).astype(out[name].dtype)
    return out
```

```python
from contextlib import ExitStack

import numpy as np

import concourse.bass as bass
from concourse import mybir

F32 = mybir.dt.float32
F32R = mybir.dt.float32r
BF16 = mybir.dt.bfloat16
F16 = mybir.dt.float16
FP8 = mybir.dt.float8e4
U32 = mybir.dt.uint32
ALU = mybir.AluOpType
ACT = mybir.ActivationFunctionType
AX = mybir.AxisListType

D = 128
TILES = 32
N = TILES * D
CH = 512
CHUNKS = N // CH
TPC = CH // D
PAIRS = CHUNKS // 2
EPS = 1e-5
EP = 40
MAXE = 36
HEADS = 16
HD = D // HEADS
GROUPS = HEADS // 4
HV = HD + 1
BIG = 1e30


class Counter:

    def __init__(self, sem, base, per, slots):
        self.sem, self.base, self.per, self.slots = sem, base, per, slots
        self.credit = per * slots

    def done(self, i):
        return i * self.per + (self.base + self.per * (1 + self.slots))

    def free(self, i):
        return i * self.per + (self.base + self.per)


class Chain:

    def __init__(self, sem):
        self.sem, self.count = sem, 0

    def __call__(self, eng, instruction):
        self.count += 1
        instruction.then_inc(self.sem, 1)
        eng.wait_ge(self.sem, self.count)


class Core:

    def __init__(self, nc, ctx):
        self.nc, self.ctx, self.counters, self.chains = nc, ctx, {}, {}
        self.passed = ctx.enter_context(nc.semaphore("s_passed"))

    def sb(self, name, shape, dt=F32, ctx=None):
        return (ctx or self.ctx).enter_context(self.nc.sbuf_tensor(name, shape, dt))

    def ps(self, name, ctx, shape=(128, CH), dt=F32):
        return ctx.enter_context(self.nc.psum_tensor(name, list(shape), dt))

    def counter(self, name, items, per=1, slots=2):
        if name not in self.counters:
            self.counters[name] = [self.ctx.enter_context(self.nc.semaphore(f"s_{name}")), 0]
        sem, base = self.counters[name]
        self.counters[name][1] += (items + slots) * per
        return Counter(sem, base, per, slots)

    def chain(self, name):
        if name not in self.chains:
            self.chains[name] = Chain(self.ctx.enter_context(self.nc.semaphore(f"s_{name}")))
        return self.chains[name]


def cols(i, n=CH):
    return bass.ds(i * n, n)


def mm3(pe, out, ah, al, bh, bl, start=True, stop=True):
    pe.matmul(out, ah, bh, start=start, stop=False)
    pe.matmul(out, ah, bl, start=False, stop=False)
    return pe.matmul(out, al, bh, start=False, stop=stop)


def spread(ap, n):
    return ap.unsqueeze(2).to_broadcast([ap.shape[0], ap.shape[1], n])


def setup_phase(k, x, ctxT, router_w, router_b, logits):
    nc = k.nc
    with ExitStack() as here:
        stage = k.sb("ctx_stage", [128, 2, CH], F32, here)
        wr = k.sb("router_w", [D, 8], F32, here)
        br = k.sb("router_b", [128, 8], F32, here)
        ps = [k.ps(f"ps_logit{u}", here) for u in range(2)]
        loaded = k.counter("loaded", 4, 16)
        arrived = [k.counter(f"arrived{u}", PAIRS, 16) for u in range(2)]
        high = k.counter("high", CHUNKS)
        low = k.counter("low", CHUNKS)
        scored = k.counter("scored", CHUNKS)
        kept = k.counter("kept", CHUNKS)
        made = k.chain("constants")
        block = here.enter_context(nc.Block())

        @block.sync
        def _(sp):
            sp.nop().then_inc(loaded.sem, loaded.credit)
            for a in arrived:
                sp.nop().then_inc(a.sem, a.credit)
            sp.dma_start(wr[:], router_w).then_inc(loaded.sem, 16)
            sp.dma_start(br[:], router_b.partition_broadcast(128)).then_inc(loaded.sem, 16)
            with sp.Fori(0, PAIRS) as it:
                for u in range(2):
                    c = it * 2 + u
                    sp.wait_ge(low.sem, low.free(c))
                    sp.sem_inc(k.passed, 1)
                    sp.wait_ge(scored.sem, scored.free(c))
                    sp.sem_inc(k.passed, 1)
                    sp.dma_start(stage[:, u], ctxT[:, cols(c)]).then_inc(arrived[u].sem, 16)
            sp.dma_start(k.X[:, :N // 2], x[:, :N // 2]).then_inc(loaded.sem, 16)
            sp.dma_start(k.X[:, N // 2:], x[:, N // 2:]).then_inc(loaded.sem, 16)
            sp.wait_ge(loaded.sem, loaded.done(3))

        @block.gpsimd
        def _(pool):
            made(pool, pool.memset(k.ident[:], 0.0))
            made(pool, pool.affine_select(out=k.ident[:], in_=k.ident[:], compare_op=ALU.not_equal, fill=1.0,
                                          base=0, pattern=[[-1, D]], channel_multiplier=1))
            made(pool, pool.tensor_copy(k.identb[:], k.ident[:]))
            made(pool, pool.memset(k.select[:], 0.0))
            sel = k.select[:].rearrange("p (e m) -> p e m", m=D)
            for part in range(3):
                made(pool, pool.affine_select(out=sel, in_=sel, compare_op=ALU.not_equal, fill=1.0,
                                              base=-EP * part, pattern=[[-1, MAXE], [0, D]], channel_multiplier=1))

        @block.vector
        def _(dve):
            for s in (high, low, kept):
                dve.nop().then_inc(s.sem, s.credit)
            dve.wait_ge(loaded.sem, loaded.done(1))
            with dve.Fori(0, PAIRS) as it:
                for u in range(2):
                    c = it * 2 + u
                    dve.wait_ge(arrived[u].sem, arrived[u].done(it))
                    hi, lo = (k.context[:, cols(c, TPC), part, :] for part in range(2))
                    tok = stage[:, u].rearrange("p (t q) -> p t q", q=D)
                    dve.tensor_copy(hi, tok).then_inc(high.sem, 1)
                    dve.wait_ge(high.sem, high.done(c))
                    dve.tensor_tensor(lo, tok, hi.bitcast(F32), ALU.subtract).then_inc(low.sem, 1)
                    dve.wait_ge(scored.sem, scored.done(c))
                    dve.tensor_tensor(
                        logits[:, cols(c, TPC * 8)].rearrange("p (t e) -> p t e", e=8),
                        ps[u][:, :TPC * 8].rearrange("p (t e) -> p t e", e=8),
                        br[:].unsqueeze(1).to_broadcast([128, TPC, 8]), ALU.add).then_inc(kept.sem, 1)

        @block.tensor
        def _(pe):
            pe.nop().then_inc(scored.sem, scored.credit)
            pe.wait_ge(loaded.sem, loaded.done(1))
            with pe.Fori(0, PAIRS) as it:
                for u in range(2):
                    c = it * 2 + u
                    pe.wait_ge(arrived[u].sem, arrived[u].done(it))
                    pe.wait_ge(kept.sem, kept.free(c))
                    for t in range(TPC):
                        last = pe.matmul(ps[u][:, 8 * t:8 * t + 8], stage[:, u, D * t:D * t + D], wr[:],
                                         start=True, stop=True, skip_group_check=True)
                    last.then_inc(scored.sem, 1)


def norm_phase(k, name, add_y=False, add_xn=False, router=None, quant=None):
    nc = k.nc
    with ExitStack() as here:
        ystage = k.sb(f"{name}_ystage", [128, 2, CH], F32, here)
        bst = k.sb(f"{name}_bst", [128, 2, TPC, 6], F32, here)
        agg = k.sb(f"{name}_agg", [128, 2, TPC, 2], F32, here)
        mv = k.sb(f"{name}_mv", [128, TILES * 2], F32, here)
        var = k.sb(f"{name}_var", [128, TILES], F32, here)
        std = k.sb(f"{name}_std", [128, TILES], F32, here)
        rstd = k.sb(f"{name}_rstd", [128, TILES], F32, here)
        xn = k.sb(f"{name}_xn", [128, 2, TPC, D], F32, here)
        xs = k.sb(f"{name}_xs", [128, 2, CH], F32, here)
        psa = [k.ps(f"{name}_psa{u}", here) for u in range(2)]
        psb = [k.ps(f"{name}_psb{u}", here) for u in range(2)]
        psl = [k.ps(f"{name}_psl{u}", here) for u in range(2)]
        staged = k.counter("staged", CHUNKS * add_y)
        returned = k.counter("returned", CHUNKS * add_y)
        added = k.counter("added", CHUNKS * add_y)
        stats = k.counter("stats", CHUNKS)
        merged = k.counter("merged", CHUNKS)
        kept_mv = k.counter("kept_mv", CHUNKS)
        var_eps = k.counter("var_eps", 1)
        rooted = k.counter("rooted", 1)
        inverted = k.counter("inverted", 1)
        normed = k.counter("normed", CHUNKS)
        turned = k.counter("turned", CHUNKS)
        taken = k.counter("taken", CHUNKS)
        high = k.counter("high", CHUNKS)
        low = k.counter("low", CHUNKS)
        scored = k.counter("scored", CHUNKS * bool(router or quant))
        kept = k.counter("kept", CHUNKS * bool(router or quant))
        rounded = k.counter("rounded", CHUNKS * bool(quant))
        xn_added = k.counter("xn_added", CHUNKS) if add_xn else None
        wquant = k.counter("wquant", int(bool(quant)))
        link = k.chain("dve_steps")
        n_loads = 0
        if router:
            wr_dram, br_dram, E, logits = router
            wr = k.sb(f"{name}_wr", [D, E], F32, here)
            br = k.sb(f"{name}_br", [128, E], F32, here)
            n_loads = 1 if br_dram is None else 2
        if quant:
            w_dram, b_dram = quant
            n_loads = 2
            wf = k.sb(f"{name}_wf", [D, D], F32, here)
            step = k.sb(f"{name}_step", [D, D], F32, here)
            wq = k.sb(f"{name}_wq", [D, D], F16, here)
            bq = k.sb(f"{name}_bq", [D, 1], F32, here)
            x8 = k.sb(f"{name}_x8", [128, 2, CH], FP8, here)
            x16 = k.sb(f"{name}_x16", [128, 2, CH], F16, here)
            o16 = k.sb(f"{name}_o16", [128, 2, CH], F16, here)
        loaded = k.counter("loaded", n_loads, 16) if n_loads else None
        block = here.enter_context(nc.Block())

        if n_loads:
            @block.sync
            def _(sp):
                sp.nop().then_inc(loaded.sem, loaded.credit)
                if router:
                    sp.dma_start(wr[:], wr_dram).then_inc(loaded.sem, 16)
                    if br_dram is not None:
                        sp.dma_start(br[:], br_dram.partition_broadcast(128)).then_inc(loaded.sem, 16)
                if quant:
                    sp.dma_start(wf[:], w_dram).then_inc(loaded.sem, 16)
                    sp.dma_start(bq[:], b_dram).then_inc(loaded.sem, 16)
                sp.wait_ge(loaded.sem, loaded.done(n_loads - 1))

        @block.scalar
        def _(act):
            for s in (staged, rooted, taken, rounded):
                act.nop().then_inc(s.sem, s.credit)
            if add_y:
                with act.Fori(0, PAIRS) as it:
                    for u in range(2):
                        c = it * 2 + u
                        act.wait_ge(returned.sem, returned.free(c))
                        act.sem_inc(k.passed, 1)
                        act.activation(ystage[:, u], k.Y[:, cols(c)], ACT.Copy).then_inc(staged.sem, 1)
            act.wait_ge(var_eps.sem, var_eps.done(0))
            act.activation(std[:], var[:], ACT.Sqrt).then_inc(rooted.sem, 1)
            with act.Fori(0, PAIRS) as it:
                for u in range(2):
                    c = it * 2 + u
                    act.wait_ge(turned.sem, turned.done(c))
                    act.wait_ge(low.sem, low.free(c))
                    if router:
                        act.wait_ge(scored.sem, scored.free(c))
                    act.activation(xs[:, u], psb[u][:], ACT.Copy).then_inc(taken.sem, 1)
                if quant:
                    for u in range(2):
                        c = it * 2 + u
                        act.wait_ge(scored.sem, scored.done(c))
                        act.wait_ge(kept.sem, kept.free(c))
                        act.activation(o16[:, u], psl[u][:], ACT.Copy).then_inc(rounded.sem, 1)

        @block.tensor
        def _(pe):
            for s in (returned, turned, scored):
                pe.nop().then_inc(s.sem, s.credit)
            if add_y:
                with pe.Fori(0, PAIRS) as it:
                    for u in range(2):
                        c = it * 2 + u
                        pe.wait_ge(staged.sem, staged.done(c))
                        pe.wait_ge(added.sem, added.free(c))
                        for t in range(TPC):
                            last = pe.transpose(psa[u][:, D * t:D * t + D], ystage[:, u, D * t:D * t + D], k.ident[:])
                        last.then_inc(returned.sem, 1)
            if n_loads:
                pe.wait_ge(loaded.sem, loaded.done(n_loads - 1))
            if quant:
                pe.wait_ge(wquant.sem, wquant.done(0))
            with pe.Fori(0, PAIRS) as it:
                for u in range(2):
                    c = it * 2 + u
                    pe.wait_ge(normed.sem, normed.done(c))
                    pe.wait_ge(taken.sem, taken.free(c))
                    for t in range(TPC):
                        last = pe.transpose(psb[u][:, D * t:D * t + D], xn[:, u, t], k.ident[:])
                    last.then_inc(turned.sem, 1)
                for u in range(2):
                    c = it * 2 + u
                    if router:
                        pe.wait_ge(taken.sem, taken.done(c))
                        pe.wait_ge(kept.sem, kept.free(c))
                        for t in range(TPC):
                            last = pe.matmul(psl[u][:, E * t:E * t + E], xs[:, u, D * t:D * t + D], wr[:],
                                             start=True, stop=True, skip_group_check=True)
                        last.then_inc(scored.sem, 1)
                    if quant:
                        pe.wait_ge(low.sem, low.done(c))
                        pe.wait_ge(rounded.sem, rounded.free(c))
                        pe.matmul(psl[u][:], wq[:], x16[:, u], start=True, stop=True).then_inc(scored.sem, 1)

        if add_xn:
            @block.gpsimd
            def _(pool):
                pool.nop().then_inc(xn_added.sem, xn_added.credit)
                with pool.Fori(0, PAIRS) as it:
                    for u in range(2):
                        c = it * 2 + u
                        pool.wait_ge(normed.sem, normed.done(c))
                        pool.tensor_tensor(k.X[:, cols(c)], k.X[:, cols(c)],
                                                        xn[:, u].rearrange("p t d -> p (t d)"), ALU.add) \
                                                            .then_inc(xn_added.sem, 1)

        @block.vector
        def _(dve):
            for s in (added, stats, merged, kept_mv, var_eps, inverted, normed, high, low, kept, wquant):
                dve.nop().then_inc(s.sem, s.credit)
            if n_loads:
                dve.wait_ge(loaded.sem, loaded.done(n_loads - 1))
            if quant:
                link(dve, dve.tensor_scalar(wf[:], wf[:], 448.0, -448.0, ALU.min, ALU.max))
                link(dve, dve.tensor_scalar(step[:].bitcast(U32), wf[:].bitcast(U32), 0x7F800000, None,
                                            ALU.bitwise_and))
                link(dve, dve.tensor_scalar(step[:], step[:], 2.0 ** -6, 1.5 * 2.0 ** 20, ALU.max, ALU.mult))
                link(dve, dve.tensor_tensor(wf[:], wf[:], step[:], ALU.add))
                dve.tensor_tensor(wq[:], wf[:], step[:], ALU.subtract).then_inc(wquant.sem, 1)
            with dve.Fori(0, PAIRS) as it:
                for u in range(2):
                    c = it * 2 + u
                    if add_y:
                        dve.wait_ge(returned.sem, returned.done(c))
                        dve.tensor_tensor(k.X[:, cols(c)], k.X[:, cols(c)], psa[u][:], ALU.add).then_inc(added.sem, 1)
                        dve.wait_ge(added.sem, added.done(c))
                    dve.wait_ge(merged.sem, merged.free(c))
                    dve.sem_inc(k.passed, 1)
                    for t in range(TPC):
                        last = dve.bn_stats(bst[:, u, t], k.X[:, bass.ds(c * CH + D * t, D)])
                    last.then_inc(stats.sem, 1)
                    dve.wait_ge(stats.sem, stats.done(c))
                    dve.wait_ge(kept_mv.sem, kept_mv.free(c))
                    dve.sem_inc(k.passed, 1)
                    for t in range(TPC):
                        last = dve.bn_aggr(agg[:, u, t], bst[:, u, t])
                    last.then_inc(merged.sem, 1)
                    dve.wait_ge(merged.sem, merged.done(c))
                    dve.tensor_copy(mv[:, cols(c, TPC * 2)], agg[:, u].rearrange("p t s -> p (t s)")) \
                        .then_inc(kept_mv.sem, 1)
            dve.wait_ge(kept_mv.sem, kept_mv.done(CHUNKS - 1))
            dve.tensor_scalar(var[:], mv[:].rearrange("p (t s) -> p t s", s=2)[:, :, 1], EPS, None,
                                          ALU.add).then_inc(var_eps.sem, 1)
            dve.wait_ge(rooted.sem, rooted.done(0))
            dve.reciprocal(rstd[:], std[:]).then_inc(inverted.sem, 1)
            dve.wait_ge(inverted.sem, inverted.done(0))
            with dve.Fori(0, PAIRS) as it:
                for u in range(2):
                    c = it * 2 + u
                    dve.wait_ge(turned.sem, turned.free(c))
                    if add_xn:
                        dve.wait_ge(xn_added.sem, xn_added.free(c))
                    for t in range(TPC):
                        last = dve.tensor_scalar(xn[:, u, t], k.X[:, bass.ds(c * CH + D * t, D)],
                                                 mv[:, bass.ds(c * (TPC * 2) + 2 * t, 1)],
                                                 rstd[:, bass.ds(c * TPC + t, 1)], ALU.subtract, ALU.mult)
                    last.then_inc(normed.sem, 1)
                for u in range(2):
                    c = it * 2 + u
                    dve.wait_ge(taken.sem, taken.done(c))
                    if quant:
                        dve.sem_inc(k.passed, 1)
                        dve.tensor_copy(x8[:, u], xs[:, u], saturate=False).then_inc(high.sem, 1)
                        dve.wait_ge(high.sem, high.done(c))
                        dve.wait_ge(scored.sem, scored.free(c))
                        dve.sem_inc(k.passed, 1)
                        dve.tensor_copy(x16[:, u], x8[:, u]).then_inc(low.sem, 1)
                    else:
                        dve.tensor_copy(k.xn[:, 0, cols(c)], xs[:, u]).then_inc(high.sem, 1)
                        dve.wait_ge(high.sem, high.done(c))
                        dve.tensor_tensor(k.xn[:, 1, cols(c)], xs[:, u], k.xn[:, 0, cols(c)].bitcast(F32),
                                                  ALU.subtract).then_inc(low.sem, 1)
                if quant:
                    for u in range(2):
                        c = it * 2 + u
                        dve.wait_ge(rounded.sem, rounded.done(c))
                        dve.tensor_scalar(k.Y[:, cols(c)], o16[:, u], bq[:], None, ALU.add).then_inc(kept.sem, 1)
                if router:
                    for u in range(2):
                        c = it * 2 + u
                        dve.wait_ge(scored.sem, scored.done(c))
                        out = logits[:, cols(c, TPC * E)]
                        if br_dram is None:
                            dve.tensor_copy(out, psl[u][:, :TPC * E]).then_inc(kept.sem, 1)
                        else:
                            dve.tensor_tensor(out.rearrange("p (t e) -> p t e", e=E),
                                                       psl[u][:, :TPC * E].rearrange("p (t e) -> p t e", e=E),
                                                       br[:].unsqueeze(1).to_broadcast([128, TPC, E]), ALU.add) \
                                                           .then_inc(kept.sem, 1)


def finish_phase(k, out):
    nc = k.nc
    with ExitStack() as here:
        ystage = k.sb("end_ystage", [128, 2, CH], F32, here)
        psa = [k.ps(f"end_psa{u}", here) for u in range(2)]
        staged = k.counter("staged", CHUNKS)
        returned = k.counter("returned", CHUNKS)
        added = k.counter("added", CHUNKS)
        stored = k.counter("stored", CHUNKS, 16)
        block = here.enter_context(nc.Block())

        @block.scalar
        def _(act):
            act.nop().then_inc(staged.sem, staged.credit)
            with act.Fori(0, PAIRS) as it:
                for u in range(2):
                    c = it * 2 + u
                    act.wait_ge(returned.sem, returned.free(c))
                    act.sem_inc(k.passed, 1)
                    act.activation(ystage[:, u], k.Y[:, cols(c)], ACT.Copy).then_inc(staged.sem, 1)

        @block.tensor
        def _(pe):
            pe.nop().then_inc(returned.sem, returned.credit)
            with pe.Fori(0, PAIRS) as it:
                for u in range(2):
                    c = it * 2 + u
                    pe.wait_ge(staged.sem, staged.done(c))
                    pe.wait_ge(added.sem, added.free(c))
                    for t in range(TPC):
                        last = pe.transpose(psa[u][:, D * t:D * t + D], ystage[:, u, D * t:D * t + D], k.ident[:])
                    last.then_inc(returned.sem, 1)

        @block.vector
        def _(dve):
            dve.nop().then_inc(added.sem, added.credit)
            with dve.Fori(0, PAIRS) as it:
                for u in range(2):
                    c = it * 2 + u
                    dve.wait_ge(returned.sem, returned.done(c))
                    dve.tensor_tensor(k.X[:, cols(c)], k.X[:, cols(c)], psa[u][:], ALU.add).then_inc(added.sem, 1)

        @block.sync
        def _(sp):
            sp.nop().then_inc(stored.sem, stored.credit)
            with sp.Fori(0, PAIRS) as it:
                for u in range(2):
                    c = it * 2 + u
                    sp.wait_ge(added.sem, added.done(c))
                    sp.sem_inc(k.passed, 1)
                    sp.dma_start(out[:, cols(c)], k.X[:, cols(c)]).then_inc(stored.sem, 16)
            sp.wait_ge(stored.sem, stored.done(CHUNKS - 1))


def route_phase(k, name, E, top, logits, rule, shared=0, bias=None, cap=None):
    nc = k.nc
    W = TILES * E
    with ExitStack() as here:
        work = k.sb(f"{name}_work", [128, W], F32, here)
        val = k.sb(f"{name}_val", [128, W], F32, here)
        eq = k.sb(f"{name}_eq", [128, W], F32, here)
        comb = k.sb(f"{name}_comb", [128, W], F32, here)
        picks = k.sb(f"{name}_picks", [128, top, W], F32, here)
        rev = k.sb(f"{name}_rev", [128, E], F32, here)
        red = k.sb(f"{name}_red", [128, TILES], F32, here)
        parts = k.sb(f"{name}_parts", [128, TILES, 3, EP], BF16, here)
        pstage = k.sb(f"{name}_pstage", [128, 2, TPC, 3 * EP], BF16, here)
        psc = [k.ps(f"{name}_psc{u}", here, (128, CH), BF16) for u in range(2)]
        br = k.sb(f"{name}_br", [128, E], F32, here) if bias is not None else None
        loaded = k.counter("loaded", 1, 16) if bias is not None else None
        curves = 2 if rule == "sigmoid" else 1
        shifted = k.counter("shifted", curves)
        curved = k.counter("curved", curves)
        split = k.counter("parts_split", 1)
        pstaged = k.counter("parts_staged", CHUNKS)
        pturned = k.counter("parts_turned", CHUNKS)
        pkept = k.counter("parts_kept", CHUNKS)
        const = k.chain("constants")
        link = k.chain("dve_steps")
        ready = k.counter("rev_ready", 1)
        masks_ready = k.counter("masks_ready", int(cap is not None))
        counted = k.counter("counted", int(cap is not None))
        if cap is not None:
            before = k.sb(f"{name}_before", [128, 128], BF16, here)
            ones = k.sb(f"{name}_ones", [128, 128], BF16, here)
            bits = k.sb(f"{name}_bits", [128, top * W], BF16, here)
            total = [k.sb(f"{name}_total{i}", [128, top * W], F32, here) for i in range(3)]
            ps_in = k.ps(f"{name}_ps_in", here)
            ps_all = k.ps(f"{name}_ps_all", here)
        block = here.enter_context(nc.Block())

        def v3(ap):
            return ap.rearrange("p (t e) -> p t e", e=E)

        @block.sync
        def _(sp):
            if bias is not None:
                sp.nop().then_inc(loaded.sem, loaded.credit)
                sp.dma_start(br[:], bias.partition_broadcast(128)).then_inc(loaded.sem, 16)
                sp.wait_ge(loaded.sem, loaded.done(0))

        @block.gpsimd
        def _(pool):
            pool.nop().then_inc(ready.sem, ready.credit)
            for e in range(E):
                last = pool.memset(rev[:, e:e + 1], float(E - e))
            const(pool, last)
            if cap is not None:
                const(pool, pool.memset(ones[:], 1.0))
                const(pool, pool.affine_select(out=before[:], in_=ones[:], compare_op=ALU.is_gt, fill=0.0,
                                               base=0, pattern=[[1, 128]], channel_multiplier=-1))
            const(pool, pool.memset(parts[:], 0.0))
            if shared:
                const(pool, pool.memset(parts[:, :, 0, E:E + shared], 1.0))
            pool.nop().then_inc(ready.sem, 1)

        @block.scalar
        def _(act):
            for s in (curved, pstaged):
                act.nop().then_inc(s.sem, s.credit)
            if rule == "sigmoid":
                act.wait_ge(shifted.sem, shifted.done(0))
                act.activation(val[:], logits[:], ACT.Sigmoid)
                act.activation(work[:], eq[:], ACT.Sigmoid).then_inc(curved.sem, 1)
                act.wait_ge(shifted.sem, shifted.done(1))
                act.activation(comb[:], comb[:], ACT.Exp).then_inc(curved.sem, 1)
            else:
                act.wait_ge(shifted.sem, shifted.done(0))
                act.activation(val[:], eq[:], ACT.Exp).then_inc(curved.sem, 1)
            act.wait_ge(split.sem, split.done(0))
            with act.Fori(0, PAIRS) as it:
                for u in range(2):
                    c = it * 2 + u
                    act.wait_ge(pturned.sem, pturned.free(c))
                    act.sem_inc(k.passed, 1)
                    act.activation(pstage[:, u].rearrange("p t r -> p (t r)"),
                                               parts[:].rearrange("p t s e -> p (t s e)")[:, cols(c, TPC * 3 * EP)],
                                               ACT.Copy).then_inc(pstaged.sem, 1)

        @block.tensor
        def _(pe):
            for s in (pturned, counted):
                pe.nop().then_inc(s.sem, s.credit)
            if cap is not None:
                pe.wait_ge(ready.sem, ready.done(0))
                pe.wait_ge(masks_ready.sem, masks_ready.done(0))
                pe.matmul(ps_in[:, :top * W], before[:], bits[:], start=True, stop=True)
                pe.matmul(ps_all[:, :top * W], ones[:], bits[:], start=True, stop=True).then_inc(counted.sem, 1)
            with pe.Fori(0, PAIRS) as it:
                for u in range(2):
                    c = it * 2 + u
                    pe.wait_ge(pstaged.sem, pstaged.done(c))
                    pe.wait_ge(pkept.sem, pkept.free(c))
                    for t in range(TPC):
                        last = pe.transpose(psc[u][:3 * EP, D * t:D * t + D], pstage[:, u, t], k.identb[:])
                    last.then_inc(pturned.sem, 1)

        @block.vector
        def _(dve):
            for s in (shifted, split, pkept, masks_ready):
                dve.nop().then_inc(s.sem, s.credit)
            if bias is not None:
                dve.wait_ge(loaded.sem, loaded.done(0))
            dve.wait_ge(ready.sem, ready.done(0))
            if rule == "sigmoid":
                dve.tensor_tensor(v3(eq[:]), v3(logits[:]),
                                              br[:].unsqueeze(1).to_broadcast([128, TILES, E]), ALU.add) \
                                                  .then_inc(shifted.sem, 1)
                dve.wait_ge(curved.sem, curved.done(0))
            else:
                link(dve, dve.tensor_reduce(red[:], v3(logits[:]), AX.X, ALU.max))
                dve.tensor_tensor(v3(eq[:]), v3(logits[:]), spread(red[:], E), ALU.subtract).then_inc(shifted.sem, 1)
                dve.wait_ge(curved.sem, curved.done(0))
                if rule == "softmax":
                    link(dve, dve.tensor_reduce(red[:], v3(val[:]), AX.X, ALU.add))
                    link(dve, dve.reciprocal(red[:], red[:]))
                    link(dve, dve.tensor_tensor(v3(val[:]), v3(val[:]), spread(red[:], E), ALU.mult))
                    link(dve, dve.tensor_copy(work[:], val[:]))
                else:
                    link(dve, dve.tensor_copy(work[:], logits[:]))
            for j in range(top):
                link(dve, dve.tensor_reduce(red[:], v3(work[:]), AX.X, ALU.max))
                link(dve, dve.tensor_tensor(v3(eq[:]), v3(work[:]), spread(red[:], E), ALU.is_equal))
                link(dve, dve.tensor_tensor(v3(eq[:]), v3(eq[:]), rev[:].unsqueeze(1).to_broadcast([128, TILES, E]),
                                            ALU.mult))
                link(dve, dve.tensor_reduce(red[:], v3(eq[:]), AX.X, ALU.max))
                link(dve, dve.tensor_tensor(v3(picks[:, j]), v3(eq[:]), spread(red[:], E), ALU.is_equal))
                if j + 1 < top:
                    link(dve, dve.scalar_tensor_tensor(work[:], picks[:, j], -BIG, work[:], ALU.mult, ALU.add))
            mask = eq
            link(dve, dve.tensor_tensor(mask[:], picks[:, 0], picks[:, 1], ALU.add))
            for j in range(2, top):
                link(dve, dve.tensor_tensor(mask[:], mask[:], picks[:, j], ALU.add))
            link(dve, dve.tensor_tensor(comb[:], val[:], mask[:], ALU.mult))
            if rule == "sigmoid":
                link(dve, dve.tensor_reduce(red[:], v3(comb[:]), AX.X, ALU.max))
                dve.tensor_tensor(v3(comb[:]), v3(comb[:]), spread(red[:], E), ALU.subtract).then_inc(shifted.sem, 1)
                dve.wait_ge(curved.sem, curved.done(1))
                link(dve, dve.tensor_tensor(comb[:], comb[:], mask[:], ALU.mult))
            link(dve, dve.tensor_reduce(red[:], v3(comb[:]), AX.X, ALU.add))
            link(dve, dve.tensor_scalar(red[:], red[:], 1e-12, None, ALU.max))
            link(dve, dve.reciprocal(red[:], red[:]))
            link(dve, dve.tensor_tensor(v3(comb[:]), v3(comb[:]), spread(red[:], E), ALU.mult))
            if cap is not None:
                dve.tensor_copy(bits[:], picks[:].rearrange("p j w -> p (j w)")).then_inc(masks_ready.sem, 1)
                dve.wait_ge(counted.sem, counted.done(0))
                link(dve, dve.tensor_copy(total[2][:], ps_all[:, :top * W]))
                link(dve, dve.tensor_copy(total[0][:], total[2][:]))
                src, dst, s = total[0], total[1], E
                while s < top * W:
                    link(dve, dve.tensor_copy(dst[:, :s], src[:, :s]))
                    link(dve, dve.tensor_tensor(dst[:, s:], src[:, s:], src[:, :top * W - s], ALU.add))
                    src, dst, s = dst, src, 2 * s
                link(dve, dve.tensor_tensor(src[:], src[:], total[2][:], ALU.subtract))
                link(dve, dve.tensor_tensor(src[:], src[:], ps_in[:, :top * W], ALU.add))
                link(dve, dve.tensor_scalar(src[:], src[:], float(cap), None, ALU.is_lt))
                link(dve, dve.tensor_tensor(src[:], src[:], picks[:].rearrange("p j w -> p (j w)"), ALU.mult))
                link(dve, dve.tensor_tensor(mask[:], src[:, :W], src[:, W:], ALU.add))
                link(dve, dve.tensor_tensor(comb[:], comb[:], mask[:], ALU.mult))
            for part in range(3):
                link(dve, dve.tensor_copy(parts[:, :, part, :E], v3(comb[:])))
                if part < 2:
                    link(dve, dve.tensor_tensor(v3(comb[:]), v3(comb[:]), parts[:, :, part, :E], ALU.subtract))
            dve.nop().then_inc(split.sem, 1)
            with dve.Fori(0, PAIRS) as it:
                for u in range(2):
                    c = it * 2 + u
                    dve.wait_ge(pturned.sem, pturned.done(c))
                    dve.tensor_copy(k.combT[:, cols(c)], psc[u][:3 * EP, :]).then_inc(pkept.sem, 1)


AHEAD = 2
STEPS = 2 * CHUNKS
ROUND = 4


def moe_phase(k, name, E, kind, w_dram, b1_dram=None, b2_dram=None):
    nc = k.nc
    glu = kind == "swiglu"
    FT = 1 if glu else 4
    W1 = 2 * D if glu else FT * D
    WC = W1 + FT * D
    Q = WC // 4
    HB = CH if glu else 2 * CH
    PER = 1 if glu else 2
    RH = ROUND if glu else 3 - 1
    func = {"relu": ACT.Relu, "gelu": ACT.Gelu, "swiglu": ACT.Silu}[kind]
    half = E // 2
    steps = E * CHUNKS
    with ExitStack() as here:
        raw = k.sb(f"{name}_raw", [128, 2, WC], F32, here)
        wh = k.sb(f"{name}_wh", [128, 2, WC], F32R, here)
        wl = k.sb(f"{name}_wl", [128, 2, WC], F32R, here)
        hf = k.sb(f"{name}_hf", [128, 2, HB], F32, here)
        gate = k.sb(f"{name}_gate", [128, 2, CH], F32, here) if glu else None
        hh = k.sb(f"{name}_hh", [128, RH, PER * HB], F32R, here)
        hl = k.sb(f"{name}_hl", [128, RH, PER * HB], F32R, here)
        share = k.sb(f"{name}_share", [128, 2, CH], F32, here)
        yt = k.sb(f"{name}_yt", [128, 2, CH], F32, here)
        psu = [k.ps(f"{name}_psu{u}", here, (128, 2 * CH)) for u in range(2)]
        psy = [k.ps(f"{name}_psy{u}", here) for u in range(2)]
        psc = [k.ps(f"{name}_psc{u}", here) for u in range(2)]
        if b1_dram is not None:
            b1 = k.sb(f"{name}_b1", [128, E * FT], F32, here)
            b2 = k.sb(f"{name}_b2", [128, E], F32, here)
        loaded = k.counter("loaded", 2 if b1_dram is not None else 0, 16)
        arrived = [k.counter(f"arrived{v}", half, 16) for v in range(2)]
        whigh = k.counter("w_high", 4 * E, slots=8)
        wsplit = k.counter("w_split", 4 * E, slots=8)
        first = k.counter("first_product", PER * steps)
        gated = k.counter("gated", steps if glu else 0)
        hidden = k.counter("hidden", PER * steps)
        hhigh = k.counter("h_high", PER * steps)
        hsplit = k.counter("h_split", PER * steps)
        second = k.counter("second_product", steps, slots=RH)
        bcast = k.counter("share_product", steps)
        shared = k.counter("share_kept", steps)
        weighed = k.counter("weighed", steps)
        summed = k.counter("summed", steps)
        cleared = k.counter("cleared", 1)
        block = here.enter_context(nc.Block())

        def sweep(eng, step):
            with eng.Fori(0, half - 1) as i:
                for j in range(STEPS):
                    step(i, j, False)
            for j in range(STEPS):
                step(half - 1, j, True)

        def ahead(i, j, last, n):
            if last and j + n >= STEPS:
                return None
            return i, j + n

        @block.sync
        def _(sp):
            sp.nop().then_inc(loaded.sem, loaded.credit)
            for a in arrived:
                sp.nop().then_inc(a.sem, a.credit)
            if b1_dram is not None:
                sp.dma_start(b1[:], b1_dram).then_inc(loaded.sem, 16)
                sp.dma_start(b2[:], b2_dram).then_inc(loaded.sem, 16)
            with sp.Fori(0, half) as i:
                for v in range(2):
                    sp.wait_ge(wsplit.sem, wsplit.free(i * 8 + (4 * v + 3)))
                    sp.sem_inc(k.passed, 1)
                    sp.dma_start(raw[:, v], w_dram[:, bass.ds(i * (2 * WC) + v * WC, WC)]) \
                        .then_inc(arrived[v].sem, 16)

        @block.gpsimd
        def _(pool):
            for s in (whigh, wsplit, summed, cleared):
                pool.nop().then_inc(s.sem, s.credit)
            pool.memset(k.Y[:], 0.0).then_inc(cleared.sem, 1)
            pool.wait_ge(cleared.sem, cleared.done(0))

            def split(i, v, q):
                n = i * 8 + (4 * v + q)
                part = slice(q * Q, q * Q + Q)
                pool.tensor_scalar(wh[:, v % 2, part], raw[:, v % 2, part], 1.0, None, ALU.mult) \
                    .then_inc(whigh.sem, 1)
                pool.wait_ge(whigh.sem, whigh.done(n))
                pool.tensor_tensor(wl[:, v % 2, part], raw[:, v % 2, part],
                                              wh[:, v % 2, part].bitcast(F32), ALU.subtract).then_inc(wsplit.sem, 1)

            pool.wait_ge(arrived[0].sem, arrived[0].done(0))
            for q in range(4):
                split(0, 0, q)

            def step(i, j, last):
                c, v = j % CHUNKS, j // CHUNKS
                if 1 <= c <= 4 and not (last and v == 1):
                    if c == 1:
                        if v == 0:
                            pool.wait_ge(arrived[1].sem, arrived[1].done(i))
                        else:
                            pool.wait_ge(arrived[0].sem, arrived[0].done(i + 1))
                        pool.wait_ge(second.sem, second.free(i * STEPS + (j - c - 1 + RH)))
                        pool.sem_inc(k.passed, 1)
                    split(i, v + 1, c - 1)
                t = i * STEPS + j
                pool.wait_ge(weighed.sem, weighed.done(t))
                pool.wait_ge(summed.sem, summed.free(t))
                pool.tensor_tensor(k.Y[:, c * CH:c * CH + CH], k.Y[:, c * CH:c * CH + CH], yt[:, j % 2],
                                              ALU.add).then_inc(summed.sem, 1)

            sweep(pool, step)

        @block.tensor
        def _(pe):
            for s in (first, second, bcast):
                pe.nop().then_inc(s.sem, s.credit)

            def up(i, j):
                c, v = j % CHUNKS, (j // CHUNKS) % 2
                t = i * STEPS + j
                xh, xl = (k.xn[:, part, c * CH:c * CH + CH] for part in range(2))
                if c == 0:
                    pe.wait_ge(wsplit.sem, wsplit.done(i * 8 + (4 * (j // CHUNKS) + 3)))
                for p in range(PER):
                    if glu:
                        pe.wait_ge(hidden.sem, hidden.free(t))
                    else:
                        pe.wait_ge(hidden.sem, hidden.free(i * (PER * STEPS) + (PER * j + p)))
                    bank = psu[j % 2 if glu else p]
                    for f in range(2):
                        w = slice((2 * p + f) * D, (2 * p + f) * D + D)
                        last = mm3(pe, bank[:, f * CH:f * CH + CH], wh[:, v, w], wl[:, v, w], xh, xl)
                    last.then_inc(first.sem, 1)

            def down(i, j):
                c, v = j % CHUNKS, j // CHUNKS
                t = i * STEPS + j
                pe.wait_ge(shared.sem, shared.free(t))
                pe.matmul(psc[j % 2][:], k.select[:, bass.ds(i * (2 * D) + v * D, D)],
                                    k.combT[:, c * CH:c * CH + CH], start=True, stop=True).then_inc(bcast.sem, 1)
                pe.wait_ge(weighed.sem, weighed.free(t))
                for p in range(PER):
                    pe.wait_ge(hsplit.sem, hsplit.done(i * (PER * STEPS) + (PER * j + p)))
                    for f in range(2 if PER == 2 else 1):
                        n = 2 * p + f
                        w = slice(W1 + n * D, W1 + n * D + D)
                        h = slice(n * CH, n * CH + CH)
                        last = mm3(pe, psy[j % 2][:], wh[:, v, w], wl[:, v, w], hh[:, j % RH, h], hl[:, j % RH, h],
                                   start=n == 0, stop=n == FT - 1)
                last.then_inc(second.sem, 1)

            ahead_of = AHEAD if glu else 1
            for j in range(ahead_of):
                up(0, j)

            def step(i, j, last):
                nxt = ahead(i, j, last, ahead_of)
                if nxt:
                    up(*nxt)
                down(i, j)

            sweep(pe, step)

        @block.scalar
        def _(act):
            for s in (shared, gated) + ((hhigh,) if glu else (hidden,)):
                act.nop().then_inc(s.sem, s.credit)
            if b1_dram is not None:
                act.wait_ge(loaded.sem, loaded.done(1))

            def front(i, j):
                t = i * STEPS + j
                if glu:
                    act.wait_ge(first.sem, first.done(t))
                    act.wait_ge(hidden.sem, hidden.free(t))
                    act.activation(gate[:, j % 2], psu[j % 2][:, :CH], func).then_inc(gated.sem, 1)
                    return
                for p in range(PER):
                    n = i * (PER * STEPS) + (PER * j + p)
                    act.wait_ge(first.sem, first.done(n))
                    act.wait_ge(hsplit.sem, hsplit.free(n))
                    act.sem_inc(k.passed, 1)
                    for f in range(2):
                        b = b1[:, bass.ds(i * (2 * FT) + (j // CHUNKS) * FT + 2 * p + f, 1)] if b1_dram is not None \
                            else 0.0
                        last = act.activation(hf[:, p, f * CH:f * CH + CH], psu[p][:, f * CH:f * CH + CH], func, bias=b)
                    last.then_inc(hidden.sem, 1)

            def high(i, j):
                t = i * STEPS + j
                act.wait_ge(hidden.sem, hidden.done(t))
                act.wait_ge(second.sem, second.free(t))
                act.activation(hh[:, j % RH], hf[:, j % 2], ACT.Copy).then_inc(hhigh.sem, 1)

            def spread_share(i, j):
                t = i * STEPS + j
                act.wait_ge(bcast.sem, bcast.done(t))
                act.wait_ge(weighed.sem, weighed.free(t))
                act.activation(share[:, j % 2], psc[j % 2][:], ACT.Copy).then_inc(shared.sem, 1)

            ahead_of = AHEAD if glu else 1
            for j in range(ahead_of):
                front(0, j)
                if glu and j == 0:
                    high(0, 0)

            def step(i, j, last):
                nxt = ahead(i, j, last, ahead_of)
                if nxt:
                    front(*nxt)
                if glu and ahead(i, j, last, 1):
                    high(i, j + 1)
                spread_share(i, j)

            sweep(act, step)

        @block.vector
        def _(dve):
            for s in (hsplit, weighed) + ((hidden,) if glu else (hhigh,)):
                dve.nop().then_inc(s.sem, s.credit)
            if b1_dram is not None:
                dve.wait_ge(loaded.sem, loaded.done(1))

            def front(i, j):
                t = i * STEPS + j
                if glu:
                    dve.wait_ge(gated.sem, gated.done(t))
                    dve.wait_ge(hsplit.sem, hsplit.free(t))
                    dve.tensor_tensor(hf[:, j % 2], gate[:, j % 2], psu[j % 2][:, CH:], ALU.mult) \
                        .then_inc(hidden.sem, 1)
                    return
                for p in range(PER):
                    n = i * (PER * STEPS) + (PER * j + p)
                    part = slice(p * HB, p * HB + HB)
                    dve.wait_ge(hidden.sem, hidden.done(n))
                    dve.wait_ge(second.sem, second.free(t))
                    dve.tensor_copy(hh[:, j % RH, part], hf[:, p]).then_inc(hhigh.sem, 1)
                    dve.wait_ge(hhigh.sem, hhigh.done(n))
                    dve.tensor_tensor(hl[:, j % RH, part], hf[:, p], hh[:, j % RH, part].bitcast(F32),
                                                 ALU.subtract).then_inc(hsplit.sem, 1)

            def low(i, j):
                t = i * STEPS + j
                dve.wait_ge(hhigh.sem, hhigh.done(t))
                dve.tensor_tensor(hl[:, j % RH], hf[:, j % 2], hh[:, j % RH].bitcast(F32), ALU.subtract) \
                    .then_inc(hsplit.sem, 1)

            def weigh(i, j):
                t = i * STEPS + j
                dve.wait_ge(second.sem, second.done(t))
                dve.wait_ge(shared.sem, shared.done(t))
                dve.wait_ge(summed.sem, summed.free(t))
                if b1_dram is not None:
                    dve.scalar_tensor_tensor(yt[:, j % 2], psy[j % 2][:],
                                                         b2[:, bass.ds(i * 2 + j // CHUNKS, 1)], share[:, j % 2],
                                                         ALU.add, ALU.mult).then_inc(weighed.sem, 1)
                else:
                    dve.tensor_tensor(yt[:, j % 2], psy[j % 2][:], share[:, j % 2], ALU.mult).then_inc(weighed.sem, 1)

            ahead_of = AHEAD if glu else 1
            for j in range(ahead_of):
                front(0, j)
                if glu and j == 0:
                    low(0, 0)

            def step(i, j, last):
                nxt = ahead(i, j, last, ahead_of)
                if nxt:
                    front(*nxt)
                if glu and ahead(i, j, last, 1):
                    low(i, j + 1)
                weigh(i, j)

            sweep(dve, step)


def attention_phase(k, name, kind, w_q=None, w_k=None, w_v=None, w_o=None, b_q=None, b_k=None, b_v=None, b_o=None,
                    ctx_tok=None):
    nc = k.nc
    stable = kind == "stablemax"
    project = w_q is not None
    scale = float(np.float32(1.0) / np.float32(np.sqrt(np.float32(HD))))
    BPC = TPC
    BODY = 2 * BPC
    NB = GROUPS if stable else 2
    with ExitStack() as here:
        stat = k.sb(f"{name}_stat", [128, 2, 2, CH], F32R, here)
        mov = k.sb(f"{name}_mov", [128, BPC, 2, D], F32R, here) if project else None
        ring = k.sb(f"{name}_ring", [128, 2, 2, 2, HEADS, D], F32R, here)
        vx = k.sb(f"{name}_vx", [128, 2, BPC, HEADS, HV], F32, here)
        vtmp = k.sb(f"{name}_vtmp", [128, CH], F32, here)
        rot = k.sb(f"{name}_rot", [128, 2, CH], F32, here)
        rs = k.sb(f"{name}_rs", [128, 2, HEADS], F32, here)
        ost = k.sb(f"{name}_ost", [128, 2, D], F32, here)
        ot = k.sb(f"{name}_ot", [128, 2, D], F32, here)
        wo = k.sb(f"{name}_wo", [D, D], F32, here)
        prob = k.Y[:].rearrange("p (s g c) -> p s g c", s=2, g=GROUPS)
        expd = k.scratch[:].rearrange("p (g c) -> p g c", g=GROUPS)
        if project:
            wraw = k.Y[:, :3 * D]
            wh = k.sb(f"{name}_wh", [D, 3 * D], F32R, here)
            wl = k.sb(f"{name}_wl", [D, 3 * D], F32R, here)
        if stable:
            ptmp = k.scratch[:, 2 * CH:3 * CH]
            bias = k.sb(f"{name}_bias", [128, 3], F32, here)
            bo = k.sb(f"{name}_bo", [128, D], F32, here)
        else:
            mx = k.sb(f"{name}_mx", [128, 2, 4], F32, here)
        pss = [k.ps(f"{name}_pss{g}", here) for g in range(NB)]
        pst = [] if stable else [k.ps(f"{name}_pst{g}", here) for g in range(2)]
        pso = [k.ps(f"{name}_pso{u}", here) for u in range(2)]
        psm = k.ps(f"{name}_psm", here)
        psr = k.ps(f"{name}_psr", here)

        n_loads = (5 if stable else 1) + (3 if project else 0)
        loaded = k.counter("loaded", n_loads, 16)
        masked = [k.counter(f"masked{s}", CHUNKS, 16 * HEADS, slots=1) for s in range(2)]
        stat_in = [k.counter(f"stat_in{u}", CHUNKS // 2 * (not project), 16, slots=1) for u in range(2)]
        v_in = k.counter("v_in", CHUNKS * (not project), 16, slots=1)
        wh_done = k.counter("proj_w_high", int(project))
        wl_done = k.counter("proj_w_low", int(project))
        zeroed = k.counter("zeroed", 2)
        pieces = k.counter("piece_product", 4 * CHUNKS * project, slots=1)
        piece_out = k.counter("piece_taken", 4 * CHUNKS * project, slots=1)
        tmp_high = k.counter("piece_high", 2 * CHUNKS * project, slots=1)
        mov_ready = k.counter("mov_ready", CHUNKS * project, slots=1)
        stat_ready = k.counter("stat_ready", CHUNKS * project)
        v_taken = k.counter("v_taken", CHUNKS * (not project), slots=1)
        score = k.counter("score", GROUPS * TILES, slots=32)
        curve = k.counter("curve", GROUPS * TILES)
        shift = k.counter("shift", GROUPS * TILES)
        exped = k.counter("exped", GROUPS * TILES)
        tposed = k.counter("tposed", GROUPS * TILES * (not stable), slots=4)
        probs = k.counter("probs", GROUPS * TILES, slots=NB)
        values = k.counter("values", TILES, slots=8)
        inverse = k.counter("inverse", TILES)
        onorm = k.counter("onorm", TILES)
        oturned = k.counter("oturned", TILES)
        otaken = k.counter("otaken", TILES)
        oproj = k.counter("oproj", TILES)
        xadded = k.counter("xadded", TILES, slots=1)
        bo_added = k.counter("bo_added", int(stable))
        block = here.enter_context(nc.Block())

        def sweep(eng, chunk_piece, scores, item):
            for q in range(4):
                chunk_piece(0, 0, q)
            for g in range(GROUPS):
                scores(0, 0, g)

            def body(i, last):
                for j in range(BODY):
                    if not (last and j >= BPC):
                        chunk_piece(i, 1 + j // BPC, j % BPC)
                    item(i, j, not (last and j == BODY - 1))

            with eng.Fori(0, CHUNKS // 2 - 1) as i:
                body(i, False)
            body(CHUNKS // 2 - 1, True)

        def chunk(i, u):
            return i * 2 + u

        def batch(i, j):
            return i * BODY + j

        def group(i, j, g):
            return i * (BODY * GROUPS) + (j * GROUPS + g)

        @block.sync
        def _(sp):
            for s in [loaded, v_in] + stat_in + masked:
                sp.nop().then_inc(s.sem, s.credit)
            if project:
                for n, w in enumerate((w_q, w_k, w_v)):
                    sp.dma_start(wraw[:, n * D:n * D + D], w).then_inc(loaded.sem, 16)
            if stable:
                for n, b in enumerate((b_q, b_k, b_v)):
                    sp.dma_start(bias[:, n:n + 1], b).then_inc(loaded.sem, 16)
                sp.dma_start(bo[:], b_o.partition_broadcast(128)).then_inc(loaded.sem, 16)
            sp.dma_start(wo[:], w_o).then_inc(loaded.sem, 16)
            sp.wait_ge(zeroed.sem, zeroed.done(0))
            with sp.Fori(0, CHUNKS // 2) as i:
                for u in range(2):
                    c = chunk(i, u)
                    if project:
                        sp.wait_ge(mov_ready.sem, mov_ready.done(c))
                        sp.sem_inc(k.passed, 1)
                        src = mov
                    else:
                        sp.wait_ge(score.sem, score.free(i * (2 * GROUPS * BPC) + (u * GROUPS * BPC + 15)))
                        sp.sem_inc(k.passed, 1)
                        sp.dma_start(stat[:, u].bitcast(F32), k.xn[:, :, cols(c)].bitcast(F32)) \
                            .then_inc(stat_in[u].sem, 16)
                        sp.wait_ge(v_taken.sem, v_taken.free(c))
                        sp.sem_inc(k.passed, 1)
                        sp.dma_start(vtmp[:], ctx_tok[:, cols(c)]).then_inc(v_in.sem, 16)
                        src = None
                    for half in range(2):
                        sp.wait_ge(score.sem, score.free(i * (4 * 8) + ((2 * u + half) * 8 + 23)))
                        sp.sem_inc(k.passed, 1)
                        for h in range(HEADS):
                            rows = slice(h * HD, h * HD + HD)
                            if src is None:
                                rows_in = k.context[rows, bass.ds(c * BPC + 2 * half, 2), :, :]
                            else:
                                rows_in = mov[rows, 2 * half:2 * half + 2, :, :]
                            sp.dma_start(ring[rows, half, :, :, h, :].rearrange("p b s q -> p (b s) q").bitcast(F32),
                                         rows_in.rearrange("p b s q -> p (b s) q").bitcast(F32)
                                         ).then_inc(masked[half].sem, 16)

        @block.gpsimd
        def _(pool):
            pool.nop().then_inc(zeroed.sem, zeroed.credit)
            pool.nop().then_inc(bo_added.sem, bo_added.credit)
            pool.memset(ring[:].rearrange("p s b l h q -> p (s b l h q)").bitcast(F32), 0.0).then_inc(zeroed.sem, 1)
            pool.memset(vx[:].rearrange("p s b h v -> p (s b h v)"), 1.0).then_inc(zeroed.sem, 1)
            if stable:
                pool.wait_ge(loaded.sem, loaded.done(n_loads - 1))
                pool.tensor_tensor(k.X[:].rearrange("p (t d) -> p t d", d=D),
                                                k.X[:].rearrange("p (t d) -> p t d", d=D),
                                                bo[:].unsqueeze(1).to_broadcast([128, TILES, D]), ALU.add) \
                                                    .then_inc(bo_added.sem, 1)

        order = (0, 1) if stable else (1, 0)

        @block.tensor
        def _(pe):
            for s in (pieces, score, tposed, values, oturned, oproj):
                pe.nop().then_inc(s.sem, s.credit)
            pe.wait_ge(loaded.sem, loaded.done(n_loads - 1))
            pe.wait_ge(zeroed.sem, zeroed.done(1))
            if project:
                pe.wait_ge(wl_done.sem, wl_done.done(0))

            def chunk_piece(i, u, q):
                if not project:
                    return
                c = chunk(i, u)
                n = i * 8 + (4 * u + q)
                pe.wait_ge(piece_out.sem, piece_out.free(n))
                if q == 3:
                    pe.wait_ge(piece_out.sem, piece_out.done(i * 8 + (4 * u + 2)))
                    for t in range(TPC):
                        last = pe.transpose(psm[:, D * t:D * t + D], vtmp[:, D * t:D * t + D], k.ident[:])
                    last.then_inc(pieces.sem, 1)
                    return
                w = order[q] if q < 2 else 2
                w = slice(w * D, w * D + D)
                if q < 2 and order[q] == 0:
                    xh, xl = (k.xn[:, part, cols(c)] for part in range(2))
                else:
                    xh, xl = (k.context[:, cols(c, TPC), part, :] for part in range(2))
                mm3(pe, psm[:], wh[:, w], wl[:, w], xh, xl).then_inc(pieces.sem, 1)

            def scores(i, j, g):
                u, b, half = (j // BPC) % 2, j % BPC, (j // 2) % 2
                if g == 0:
                    if project:
                        pe.wait_ge(stat_ready.sem, stat_ready.done(i * 2 + j // BPC))
                    else:
                        pe.wait_ge(stat_in[u].sem, stat_in[u].done(i + j // BODY))
                    pe.wait_ge(masked[half].sem, masked[half].done(i * 2 + j // BPC))
                pe.wait_ge((probs if stable else shift).sem, (probs if stable else shift).free(group(i, j, g)))
                a = slice(b * D, b * D + D)
                m = ring[:, half, b % 2, :, 4 * g:4 * g + 4, :].rearrange("p l h q -> p l (h q)")
                mm3(pe, pss[g % NB][:], stat[:, u, 0, a], stat[:, u, 1, a], m[:, 0], m[:, 1]).then_inc(score.sem, 1)

            def tpose(i, j, g):
                n = group(i, j, g)
                pe.wait_ge(exped.sem, exped.done(n))
                pe.wait_ge(probs.sem, probs.free(n))
                for h in range(4):
                    last = pe.transpose(pst[g % 2][:, D * h:D * h + D], expd[:, g, D * h:D * h + D], k.ident[:])
                last.then_inc(tposed.sem, 1)

            def times_v(i, j, g):
                u, b = j // BPC, j % BPC
                n = batch(i, j)
                if g == 0:
                    if project:
                        pe.wait_ge(piece_out.sem, piece_out.done(i * 8 + (4 * u + 3)))
                    else:
                        pe.wait_ge(v_taken.sem, v_taken.done(chunk(i, u)))
                    pe.wait_ge(onorm.sem, onorm.free(n))
                pe.wait_ge(probs.sem, probs.done(group(i, j, g)))
                for h in range(4 * g, 4 * g + 4):
                    last = pe.matmul(pso[j % 2][:, HV * h:HV * h + HV], prob[:, j % 2, g, D * (h % 4):D * (h % 4) + D],
                                     vx[:, u, b, h], start=True, stop=True, skip_group_check=True)
                if g == GROUPS - 1:
                    last.then_inc(values.sem, 1)

            def turn(i, j):
                pe.wait_ge(onorm.sem, onorm.done(batch(i, j)))
                pe.wait_ge(xadded.sem, xadded.free(batch(i, j)))
                pe.transpose(psr[:, :D], ost[:, j % 2], k.ident[:]).then_inc(oturned.sem, 1)

            def out(i, j):
                pe.wait_ge(otaken.sem, otaken.done(batch(i, j)))
                pe.matmul(psr[:, D:2 * D], ot[:, j % 2], wo[:], start=True, stop=True,
                                    skip_group_check=True).then_inc(oproj.sem, 1)

            def item(i, j, more):
                for g in range(GROUPS):
                    if more:
                        scores(i, j + 1, g)
                    if not stable:
                        tpose(i, j, g)
                    if g == 0 and j > 0:
                        turn(i, j - 1)
                    if g > 0:
                        times_v(i, j, g - 1)
                    if g == 2 and j > 0:
                        out(i, j - 1)
                times_v(i, j, GROUPS - 1)
                if j == BODY - 1:
                    turn(i, j)
                    out(i, j)

            sweep(pe, chunk_piece, scores, item)

        @block.scalar
        def _(act):
            for s in (exped, otaken) + ((curve,) if stable else (probs,)):
                act.nop().then_inc(s.sem, s.credit)
            if stable:
                nc.scalar.preload_act_table_set("natural_log_exp_and_others")
                act.wait_ge(loaded.sem, loaded.done(n_loads - 1))

            def chunk_piece(i, u, q):
                if q != 2 or not project:
                    return
                n = i * 8 + (4 * u + q)
                act.wait_ge(pieces.sem, pieces.done(n))
                act.wait_ge(piece_out.sem, piece_out.free(n))
                if stable:
                    act.activation(vtmp[:], psm[:], ACT.Identity, bias=bias[:, 2:3]).then_inc(piece_out.sem, 1)
                else:
                    act.activation(vtmp[:], psm[:], ACT.Copy).then_inc(piece_out.sem, 1)

            def scores(i, j, g):
                n = group(i, j, g)
                act.wait_ge(shift.sem, shift.done(n))
                if stable:
                    act.wait_ge(probs.sem, probs.free(i * (BODY * GROUPS) + (j * GROUPS + g + 2)))
                    act.activation(expd[:, g % 2], rot[:, g % 2], ACT.Ln, bias=1.0).then_inc(curve.sem, 1)
                    act.wait_ge(curve.sem, curve.done(n))
                    act.activation(expd[:, g % 2], expd[:, g % 2], ACT.Exp, scale=-1.0).then_inc(exped.sem, 1)
                else:
                    act.wait_ge(tposed.sem, tposed.free(n))
                    act.activation(expd[:, g], rot[:, g % 2], ACT.Exp, scale=scale).then_inc(exped.sem, 1)

            def take(i, j):
                act.wait_ge(oturned.sem, oturned.done(batch(i, j)))
                act.wait_ge(oproj.sem, oproj.free(batch(i, j)))
                act.activation(ot[:, j % 2], psr[:, :D], ACT.Copy).then_inc(otaken.sem, 1)

            def item(i, j, more):
                for g in range(GROUPS):
                    if not stable:
                        act.wait_ge(tposed.sem, tposed.done(group(i, j, g)))
                        act.wait_ge(values.sem, values.free(i * BODY + (j + 6)))
                        act.activation(prob[:, j % 2, g], pst[g % 2][:], ACT.Copy).then_inc(probs.sem, 1)
                    if g == 1 and j > 0:
                        take(i, j - 1)
                    if more:
                        scores(i, j + 1, g)
                if j == BODY - 1:
                    take(i, j)

            sweep(act, chunk_piece, scores, item)

        @block.vector
        def _(dve):
            for s in (wh_done, wl_done, piece_out, tmp_high, mov_ready, stat_ready, v_taken, shift, inverse,
                      onorm, xadded) + ((probs,) if stable else (curve,)):
                dve.nop().then_inc(s.sem, s.credit)
            dve.wait_ge(loaded.sem, loaded.done(n_loads - 1))
            dve.wait_ge(zeroed.sem, zeroed.done(1))
            if project:
                dve.tensor_copy(wh[:], wraw).then_inc(wh_done.sem, 1)
                dve.wait_ge(wh_done.sem, wh_done.done(0))
                dve.tensor_tensor(wl[:], wraw, wh[:].bitcast(F32), ALU.subtract).then_inc(wl_done.sem, 1)
                dve.wait_ge(wl_done.sem, wl_done.done(0))
            if stable:
                dve.wait_ge(bo_added.sem, bo_added.done(0))

            def chunk_piece(i, u, q):
                c = chunk(i, u)
                n = i * 8 + (4 * u + q)
                if q == 2:
                    return
                if q == 3:
                    dve.wait_ge(values.sem, values.free(i * (2 * BPC) + (u * BPC + 3)))
                    if project:
                        dve.wait_ge(pieces.sem, pieces.done(n))
                        src = psm[:]
                    else:
                        dve.wait_ge(v_in.sem, v_in.done(c))
                        src = vtmp[:]
                    ins = dve.tensor_copy(vx[:, u % 2, :, :, 0:HD], src.rearrange("p (b h d) -> p b h d", b=BPC, h=HEADS))
                    ins.then_inc((piece_out if project else v_taken).sem, 1)
                    return
                if not project:
                    return
                dve.wait_ge(pieces.sem, pieces.done(n))
                if q == 0:
                    for m in masked:
                        dve.wait_ge(m.sem, m.free(c))
                    hi, lo, ready = mov[:, :, 0, :], mov[:, :, 1, :], mov_ready
                else:
                    dve.wait_ge(score.sem, score.free(i * (2 * GROUPS * BPC) + (u * GROUPS * BPC + 15)))
                    hi, lo = (stat[:, u % 2, part].rearrange("p (t q) -> p t q", q=D) for part in range(2))
                    ready = stat_ready
                src = psm[:]
                if stable:
                    if q == 0:
                        dve.wait_ge(stat_ready.sem, stat_ready.free(i * 2 + (u + 1)))
                    else:
                        dve.wait_ge(mov_ready.sem, mov_ready.done(c))
                    dve.tensor_scalar(ptmp, psm[:], bias[:, q:q + 1], scale if q == 0 else 1.0,
                                                    ALU.add, ALU.mult).then_inc(piece_out.sem, 1)
                    dve.wait_ge(piece_out.sem, piece_out.done(n))
                    src = ptmp
                src = src.rearrange("p (t q) -> p t q", q=D)
                m = i * 4 + (2 * u + q)
                dve.tensor_copy(hi, src).then_inc(tmp_high.sem, 1)
                dve.wait_ge(tmp_high.sem, tmp_high.done(m))
                dve.tensor_tensor(lo, src, hi.bitcast(F32), ALU.subtract).then_inc(ready.sem, 1)
                if not stable:
                    dve.wait_ge(ready.sem, ready.done(c))
                    dve.nop().then_inc(piece_out.sem, 1)

            def front(i, j, g):
                n = group(i, j, g)
                dve.wait_ge(score.sem, score.done(n))
                if stable:
                    dve.wait_ge(curve.sem, curve.free(n))
                    dve.tensor_scalar(rot[:, g % 2], pss[g][:], -1.0, 0.0, ALU.mult, ALU.max).then_inc(shift.sem, 1)
                    return
                s3 = pss[g % 2][:].rearrange("p (h q) -> p h q", h=4)
                dve.wait_ge(shift.sem, shift.free(n))
                dve.tensor_reduce(mx[:, g % 2], s3, AX.X, ALU.max).then_inc(curve.sem, 1)
                dve.wait_ge(curve.sem, curve.done(n))
                dve.wait_ge(exped.sem, exped.free(n))
                dve.tensor_tensor(rot[:, g % 2].rearrange("p (h q) -> p h q", h=4), s3,
                                            spread(mx[:, g % 2], D), ALU.subtract).then_inc(shift.sem, 1)

            def back(i, j, g):
                dve.wait_ge(exped.sem, exped.done(group(i, j, g)))
                dve.wait_ge(values.sem, values.free(i * BODY + (j + 6)))
                dve.scalar_tensor_tensor(prob[:, j % 2, g], pss[g][:], 0.0, expd[:, g % 2],
                                                   ALU.max, ALU.add).then_inc(probs.sem, 1)

            def scores(i, j, g):
                front(i, j, g)
                if stable and g > 0:
                    back(i, j, g - 1)
                if stable and g == GROUPS - 1:
                    back(i, j, g)

            def normalise(i, j):
                n = batch(i, j)
                dve.wait_ge(values.sem, values.done(n))
                o = pso[j % 2][:, :HEADS * HV].rearrange("p (h v) -> p h v", v=HV)
                dve.wait_ge(onorm.sem, onorm.free(n))
                dve.reciprocal(rs[:, j % 2], o[:, :, HD]).then_inc(inverse.sem, 1)
                dve.wait_ge(inverse.sem, inverse.done(n))
                dve.wait_ge(oturned.sem, oturned.free(n))
                dve.tensor_tensor(ost[:, j % 2].rearrange("p (h d) -> p h d", d=HD), o[:, :, :HD],
                                            spread(rs[:, j % 2], HD), ALU.mult).then_inc(onorm.sem, 1)

            def add(i, j):
                n = batch(i, j)
                dve.wait_ge(oproj.sem, oproj.done(n))
                dve.tensor_tensor(k.X[:, cols(n, D)], k.X[:, cols(n, D)], psr[:, D:2 * D], ALU.add) \
                    .then_inc(xadded.sem, 1)

            def item(i, j, more):
                for g in range(GROUPS):
                    if g == 3 and j > 0:
                        add(i, j - 1)
                    if more:
                        scores(i, j + 1, g)
                normalise(i, j)
                if j == BODY - 1:
                    add(i, j)

            sweep(dve, chunk_piece, scores, item)


def network(nc, a, out):
    with ExitStack() as ctx:
        k = Core(nc, ctx)
        k.X = k.sb("X", [128, N])
        k.Y = k.sb("Y", [128, N])
        k.xn = k.sb("xn", [128, 2, N], F32R)
        k.context = k.sb("context", [128, TILES, 2, D], F32R)
        k.scratch = k.sb("scratch", [128, N // 2])
        k.combT = k.scratch[:].bitcast(BF16)[:3 * EP, :]
        k.select = k.sb("select", [3 * EP, MAXE * D], BF16)
        k.ident = k.sb("ident", [D, D])
        k.identb = k.sb("identb", [D, D], BF16)

        def logits(E):
            return k.scratch[:, :TILES * E]

        setup_phase(k, a["x"], a["ctxT"], a["L0x_Wg"], a["L0x_bg"], logits(8))
        route_phase(k, "r0", 8, 2, logits(8), "logits")
        norm_phase(k, "n0")
        moe_phase(k, "m0", 8, "relu", a["L0x_w"], a["L0x_b1"], a["L0x_b2"])
        norm_phase(k, "n1", add_y=True, add_xn=True, router=(a["L0f_cT"], None, 8, logits(8)))
        route_phase(k, "r1", 8, 2, logits(8), "sigmoid", shared=2, bias=a["L0f_rb"])
        moe_phase(k, "m1", 10, "gelu", a["L0f_w"])
        norm_phase(k, "n2", add_y=True)
        attention_phase(k, "a1", "stablemax", *(a[f"L1x_W{w}"] for w in "qkvo"), *(a[f"L1x_b{w}"] for w in "qkvo"))
        norm_phase(k, "n3", router=(a["L1f_gT"], None, 8, logits(8)))
        route_phase(k, "r3", 8, 2, logits(8), "softmax", cap=2 * N // 8)
        moe_phase(k, "m3", 8, "relu", a["L1f_w"], a["L1f_b1"], a["L1f_b2"])
        norm_phase(k, "n4", add_y=True)
        attention_phase(k, "a2", "softmax", w_o=a["L2x_Wo"], ctx_tok=a["ctx_tok"])
        norm_phase(k, "n5", quant=(a["L2f_wT"], a["L2f_b"]))
        norm_phase(k, "n6", add_y=True)
        attention_phase(k, "a3", "softmax", *(a[f"L3x_W{w}"] for w in "qkvo"))
        norm_phase(k, "n7", router=(a["L3f_rT"], a["L3f_rb"], 32, logits(32)))
        route_phase(k, "r7", 32, 4, logits(32), "softmax", shared=4)
        moe_phase(k, "m7", 36, "swiglu", a["L3f_w"])
        finish_phase(k, out)


def _lay_out(v):
    v = {n: np.asarray(a) for n, a in v.items()}

    def tokens(x):
        return x.reshape(TILES, D, D).transpose(1, 0, 2).reshape(D, N)

    def first(w):
        return w.transpose(1, 0, 2)

    def second(w):
        e, f, d = w.shape
        return w.reshape(e, f // D, D, d).transpose(2, 0, 1, 3).reshape(D, e, f // D * d)

    def pack(*parts):
        return np.concatenate(parts, axis=2).reshape(D, -1)

    def bias1(b):
        return b.reshape(8, 4, D).transpose(2, 0, 1).reshape(D, 32)

    def heads(w):
        return w.transpose(1, 0, 2).reshape(D, D)

    def t(w):
        return w.swapaxes(-1, -2)

    def cut(w):
        return w.reshape(4, D, D)

    fc = np.concatenate([v["L0_ffn_Wfc_r"], v["L0_ffn_Wfc_sh"]])
    proj = np.concatenate([v["L0_ffn_Wproj_r"], v["L0_ffn_Wproj_sh"]])
    gate = np.concatenate([v["L3_ffn_gate_w"], cut(v["L3_ffn_sgate_w"])])
    up = np.concatenate([v["L3_ffn_up_w"], cut(v["L3_ffn_sup_w"])])
    down = np.concatenate([t(v["L3_ffn_down_w"]), cut(t(v["L3_ffn_sdown_w"]))])
    laid = {
        "x": tokens(v["x"]), "ctxT": v["ctx_1024"].reshape(N, D).T, "ctx_tok": tokens(v["ctx_1024"]),
        "L0x_Wg": v["L0_xattn_Wg"], "L0x_bg": v["L0_xattn_bg"],
        "L0x_w": pack(first(v["L0_xattn_W1"]), second(v["L0_xattn_W2"])),
        "L0x_b1": bias1(v["L0_xattn_b1"]), "L0x_b2": v["L0_xattn_b2"].T,
        "L0f_cT": v["L0_ffn_centroids"].T, "L0f_rb": v["L0_ffn_routing_bias"],
        "L0f_w": pack(first(t(fc)), second(t(proj))),
        **{f"L1x_W{w}": v[f"L1_xattn_W{w}"].T for w in "qkvo"},
        **{f"L1x_b{w}": v[f"L1_xattn_b{w}"].reshape(D, 1) for w in "qkv"}, "L1x_bo": v["L1_xattn_bo"],
        "L1f_gT": v["L1_ffn_gate_w"].T,
        "L1f_w": pack(first(t(v["L1_ffn_fc1_w"])), second(v["L1_ffn_fc2_w"])),
        "L1f_b1": bias1(v["L1_ffn_fc1_b"]), "L1f_b2": v["L1_ffn_fc2_b"].reshape(8, D).T,
        "L2x_Wo": v["L2_xattn_w_concat"].T, "L2f_wT": v["L2_ffn_weight"].T, "L2f_b": v["L2_ffn_bias"].reshape(D, 1),
        **{f"L3x_W{w}": heads(v[f"L3_xattn_W{w}"]) for w in "qkv"}, "L3x_Wo": v["L3_xattn_Wo"].T,
        "L3f_rT": v["L3_ffn_router_w"].T, "L3f_rb": v["L3_ffn_router_bias"],
        "L3f_w": pack(first(t(gate)), first(t(up)), second(down)),
    }
    return {f"in_{n}": np.ascontiguousarray(a) for n, a in laid.items()}


def kernel(**inputs):
    import concourse.bacc as bacc
    from concourse.bass_utils import run_bass_kernel_spmd

    nc = bacc.Bacc("TRN2", target_bir_lowering=False, num_devices=1)
    arrays = _lay_out(inputs)
    aps = {n[3:]: nc.dram_tensor(n, a.shape, mybir.dt.from_np(a.dtype), kind="ExternalInput").ap()
           for n, a in arrays.items()}
    out = nc.dram_tensor("out_x", (D, N), F32, kind="ExternalOutput").ap()
    network(nc, aps, out)
    result = run_bass_kernel_spmd(nc, [arrays], core_ids=[0])
    got = np.asarray(result.results[0]["out_x"])
    return np.ascontiguousarray(got.reshape(D, TILES, D).transpose(1, 0, 2))
```

```python
from contextlib import ExitStack

import numpy as np

import concourse.bass as bass
from concourse import mybir

F32 = mybir.dt.float32
F32R = mybir.dt.float32r
BF16 = mybir.dt.bfloat16
F16 = mybir.dt.float16
FP8 = mybir.dt.float8e4
U32 = mybir.dt.uint32
ALU = mybir.AluOpType
ACT = mybir.ActivationFunctionType
AX = mybir.AxisListType

D = 128
TILES = 32
N = TILES * D
CH = 512
CHUNKS = N // CH
TPC = CH // D
PAIRS = CHUNKS // 2
EPS = 1e-5
EP = 40
MAXE = 36
HEADS = 16
HD = D // HEADS
PIECES = 3
GROUPS = HEADS // 4
OCT = 8
HR = D // OCT
BIG = 1e30


class Counter:

    def __init__(self, sem, base, per, slots):
        self.sem, self.base, self.per, self.slots = sem, base, per, slots
        self.credit = per * slots

    def done(self, i):
        return i * self.per + (self.base + self.per * (1 + self.slots))

    def free(self, i):
        return i * self.per + (self.base + self.per)


class Chain:

    def __init__(self, sem):
        self.sem, self.count = sem, 0

    def __call__(self, eng, instruction):
        self.count += 1
        instruction.then_inc(self.sem, 1)
        eng.wait_ge(self.sem, self.count)


class Core:

    def __init__(self, nc, ctx):
        self.nc, self.ctx, self.counters, self.chains = nc, ctx, {}, {}
        self.passed = ctx.enter_context(nc.semaphore("s_passed"))

    def sb(self, name, shape, dt=F32, ctx=None):
        return (ctx or self.ctx).enter_context(self.nc.sbuf_tensor(name, shape, dt))

    def ps(self, name, ctx, shape=(128, CH), dt=F32):
        return ctx.enter_context(self.nc.psum_tensor(name, list(shape), dt))

    def counter(self, name, items, per=1, slots=2):
        if name not in self.counters:
            self.counters[name] = [self.ctx.enter_context(self.nc.semaphore(f"s_{name}")), 0]
        sem, base = self.counters[name]
        self.counters[name][1] += (items + slots) * per
        return Counter(sem, base, per, slots)

    def chain(self, name):
        if name not in self.chains:
            self.chains[name] = Chain(self.ctx.enter_context(self.nc.semaphore(f"s_{name}")))
        return self.chains[name]


def cols(i, n=CH):
    return bass.ds(i * n, n)


def mm3(pe, out, ah, al, bh, bl, start=True, stop=True):
    pe.matmul(out, ah, bh, start=start, stop=False)
    pe.matmul(out, ah, bl, start=False, stop=False)
    return pe.matmul(out, al, bh, start=False, stop=stop)


def spread(ap, n):
    return ap.unsqueeze(2).to_broadcast([ap.shape[0], ap.shape[1], n])


class Weights:

    def __init__(self, k, name, kind, w_dram, ctx):
        self.columns = 3 * D if kind == "swiglu" else 8 * D
        self.w_dram = w_dram
        self.raw = k.sb(f"{name}_raw", [128, 2, self.columns], F32, ctx)
        self.wh = k.sb(f"{name}_wh", [128, 2, self.columns], F32R, ctx)
        self.wl = k.sb(f"{name}_wl", [128, 2, self.columns], F32R, ctx)
        self.fetched = [k.counter(f"fetched{v}", 1, 16) for v in range(2)]
        self.first_high = k.counter("first_high", 1)
        self.first_split = k.counter("first_split", 1)

    def fetch(self, sp):
        for v in range(2):
            there = self.fetched[v]
            sp.nop().then_inc(there.sem, there.credit)
            sp.dma_start(self.raw[:, v], self.w_dram[:, v * self.columns:(v + 1) * self.columns]) \
                .then_inc(there.sem, 16)

    def split_first(self, pool):
        there, high, both = self.fetched[0], self.first_high, self.first_split
        pool.nop().then_inc(high.sem, high.credit)
        pool.nop().then_inc(both.sem, both.credit)
        pool.wait_ge(there.sem, there.done(0))
        pool.tensor_scalar(self.wh[:, 0], self.raw[:, 0], 1.0, None, ALU.mult).then_inc(high.sem, 1)
        pool.wait_ge(high.sem, high.done(0))
        pool.tensor_tensor(self.wl[:, 0], self.raw[:, 0], self.wh[:, 0].bitcast(F32), ALU.subtract) \
            .then_inc(both.sem, 1)


def make_select(k, pool):
    made = k.chain("constants")
    sel = k.select[:3 * EP].rearrange("p (e m) -> p e m", m=D)
    made(pool, pool.memset(k.select[:], 0.0))
    for part in range(3):
        made(pool, pool.affine_select(out=sel, in_=sel, compare_op=ALU.not_equal, fill=1.0,
                                      base=-EP * part, pattern=[[-1, MAXE], [0, D]], channel_multiplier=1))


def setup_phase(k, x, ctxT, router_w, router_b, logits):
    nc = k.nc
    with ExitStack() as here:
        stage = k.sb("ctx_stage", [128, 2, CH], F32, here)
        wr = k.sb("router_w", [D, 8], F32, here)
        br = k.sb("router_b", [128, 8], F32, here)
        ps = [k.ps(f"ps_logit{u}", here) for u in range(2)]
        loaded = k.counter("loaded", 4, 16)
        arrived = [k.counter(f"arrived{u}", PAIRS, 16) for u in range(2)]
        high = k.counter("high", CHUNKS)
        low = k.counter("low", CHUNKS)
        scored = k.counter("scored", CHUNKS)
        kept = k.counter("kept", CHUNKS)
        made = k.chain("constants")
        block = here.enter_context(nc.Block())

        @block.sync
        def _(sp):
            sp.nop().then_inc(loaded.sem, loaded.credit)
            for a in arrived:
                sp.nop().then_inc(a.sem, a.credit)
            sp.dma_start(wr[:], router_w).then_inc(loaded.sem, 16)
            sp.dma_start(br[:], router_b.partition_broadcast(128)).then_inc(loaded.sem, 16)
            with sp.Fori(0, PAIRS) as it:
                for u in range(2):
                    c = it * 2 + u
                    sp.wait_ge(low.sem, low.free(c))
                    sp.sem_inc(k.passed, 1)
                    sp.wait_ge(scored.sem, scored.free(c))
                    sp.sem_inc(k.passed, 1)
                    sp.dma_start(stage[:, u], ctxT[:, cols(c)]).then_inc(arrived[u].sem, 16)
            sp.dma_start(k.X[:, :N // 2], x[:, :N // 2]).then_inc(loaded.sem, 16)
            sp.dma_start(k.X[:, N // 2:], x[:, N // 2:]).then_inc(loaded.sem, 16)
            sp.wait_ge(loaded.sem, loaded.done(3))

        @block.gpsimd
        def _(pool):
            made(pool, pool.memset(k.ident[:], 0.0))
            made(pool, pool.affine_select(out=k.ident[:], in_=k.ident[:], compare_op=ALU.not_equal, fill=1.0,
                                          base=0, pattern=[[-1, D]], channel_multiplier=1))
            made(pool, pool.tensor_copy(k.identb[:], k.ident[:]))

        @block.vector
        def _(dve):
            for s in (high, low, kept):
                dve.nop().then_inc(s.sem, s.credit)
            dve.wait_ge(loaded.sem, loaded.done(1))
            with dve.Fori(0, PAIRS) as it:
                for u in range(2):
                    c = it * 2 + u
                    dve.wait_ge(arrived[u].sem, arrived[u].done(it))
                    hi, lo = (k.context[:, cols(c, TPC), part, :] for part in range(2))
                    tok = stage[:, u].rearrange("p (t q) -> p t q", q=D)
                    dve.tensor_copy(hi, tok).then_inc(high.sem, 1)
                    dve.wait_ge(high.sem, high.done(c))
                    dve.tensor_tensor(lo, tok, hi.bitcast(F32), ALU.subtract).then_inc(low.sem, 1)
                    dve.wait_ge(scored.sem, scored.done(c))
                    dve.tensor_tensor(
                        logits[:, cols(c, TPC * 8)].rearrange("p (t e) -> p t e", e=8),
                        ps[u][:, :TPC * 8].rearrange("p (t e) -> p t e", e=8),
                        br[:].unsqueeze(1).to_broadcast([128, TPC, 8]), ALU.add).then_inc(kept.sem, 1)

        @block.tensor
        def _(pe):
            pe.nop().then_inc(scored.sem, scored.credit)
            pe.wait_ge(loaded.sem, loaded.done(1))
            with pe.Fori(0, PAIRS) as it:
                for u in range(2):
                    c = it * 2 + u
                    pe.wait_ge(arrived[u].sem, arrived[u].done(it))
                    pe.wait_ge(kept.sem, kept.free(c))
                    for t in range(TPC):
                        last = pe.matmul(ps[u][:, 8 * t:8 * t + 8], stage[:, u, D * t:D * t + D], wr[:],
                                         start=True, stop=True, skip_group_check=True)
                    last.then_inc(scored.sem, 1)


def norm_phase(k, name, add_y=False, add_xn=False, router=None, quant=None, new_select=False,
               weights=None):
    nc = k.nc
    with ExitStack() as here:
        ystage = k.sb(f"{name}_ystage", [128, 2, CH], F32, here)
        bst = k.sb(f"{name}_bst", [128, 2, TPC, 6], F32, here)
        agg = k.sb(f"{name}_agg", [128, 2, TPC, 2], F32, here)
        mv = k.sb(f"{name}_mv", [128, TILES * 2], F32, here)
        var = k.sb(f"{name}_var", [128, TILES], F32, here)
        std = k.sb(f"{name}_std", [128, TILES], F32, here)
        rstd = k.sb(f"{name}_rstd", [128, TILES], F32, here)
        xn = k.sb(f"{name}_xn", [128, 4, TPC, D], F32, here)
        xs = k.sb(f"{name}_xs", [128, 2, CH], F32, here)
        psa = [k.ps(f"{name}_psa{u}", here) for u in range(2)]
        psb = [k.ps(f"{name}_psb{u}", here) for u in range(2)]
        psl = [k.ps(f"{name}_psl{u}", here) for u in range(2)]
        staged = k.counter("staged", CHUNKS * add_y)
        returned = k.counter("returned", CHUNKS * add_y)
        added = k.counter("added", CHUNKS * add_y)
        stats = k.counter("stats", CHUNKS)
        merged = k.counter("merged", CHUNKS)
        kept_mv = k.counter("kept_mv", CHUNKS)
        var_eps = k.counter("var_eps", 1)
        rooted = k.counter("rooted", 1)
        inverted = k.counter("inverted", 1)
        normed = k.counter("normed", CHUNKS, slots=4)
        turned = k.counter("turned", CHUNKS, slots=4)
        taken = k.counter("taken", CHUNKS)
        high = k.counter("high", CHUNKS)
        low = k.counter("low", CHUNKS)
        scored = k.counter("scored", CHUNKS * bool(router or quant))
        kept = k.counter("kept", CHUNKS * bool(router or quant))
        rounded = k.counter("rounded", CHUNKS * bool(quant))
        xn_added = k.counter("xn_added", CHUNKS, slots=4) if add_xn else None
        wquant = k.counter("wquant", int(bool(quant)))
        link = k.chain("dve_steps")
        n_loads = 0
        if router:
            wr_dram, br_dram, E, logits = router
            wr = k.sb(f"{name}_wr", [D, E], F32, here)
            br = k.sb(f"{name}_br", [128, E], F32, here)
            n_loads = 1 if br_dram is None else 2
        if quant:
            w_dram, b_dram = quant
            n_loads = 2
            wf = k.sb(f"{name}_wf", [D, D], F32, here)
            step = k.sb(f"{name}_step", [D, D], F32, here)
            wq = k.sb(f"{name}_wq", [D, D], F16, here)
            bq = k.sb(f"{name}_bq", [D, 1], F32, here)
            x8 = k.sb(f"{name}_x8", [128, 2, CH], FP8, here)
            x16 = k.sb(f"{name}_x16", [128, 2, CH], F16, here)
            o16 = k.sb(f"{name}_o16", [128, 2, CH], F16, here)
        loaded = k.counter("loaded", n_loads, 16) if n_loads else None
        block = here.enter_context(nc.Block())

        if weights:
            @block.sync
            def _(sp):
                weights.fetch(sp)

        if n_loads:
            @block.sync
            def _(sp):
                sp.nop().then_inc(loaded.sem, loaded.credit)
                if router:
                    sp.dma_start(wr[:], wr_dram).then_inc(loaded.sem, 16)
                    if br_dram is not None:
                        sp.dma_start(br[:], br_dram.partition_broadcast(128)).then_inc(loaded.sem, 16)
                if quant:
                    sp.dma_start(wf[:], w_dram).then_inc(loaded.sem, 16)
                    sp.dma_start(bq[:], b_dram).then_inc(loaded.sem, 16)
                sp.wait_ge(loaded.sem, loaded.done(n_loads - 1))

        @block.scalar
        def _(act):
            for s in (staged, rooted, taken, rounded) + (() if quant else (high,)):
                act.nop().then_inc(s.sem, s.credit)
            nc.scalar.preload_act_table_set("sqrt_and_others")
            if add_y:
                with act.Fori(0, PAIRS) as it:
                    for u in range(2):
                        c = it * 2 + u
                        act.wait_ge(returned.sem, returned.free(c))
                        act.sem_inc(k.passed, 1)
                        act.activation(ystage[:, u], k.Y[:, cols(c)], ACT.Copy).then_inc(staged.sem, 1)
            act.wait_ge(var_eps.sem, var_eps.done(0))
            act.activation(std[:], var[:], ACT.Sqrt).then_inc(rooted.sem, 1)
            with act.Fori(0, PAIRS) as it:
                for u in range(2):
                    c = it * 2 + u
                    act.wait_ge(turned.sem, turned.done(c))
                    act.wait_ge(low.sem, low.free(c))
                    if router:
                        act.wait_ge(scored.sem, scored.free(c))
                    act.activation(xs[:, u], psb[u][:], ACT.Copy).then_inc(taken.sem, 1)
                    if not quant:
                        act.sem_inc(k.passed, 1)
                        act.activation(k.xn[:, 0, cols(c)], psb[u][:], ACT.Copy).then_inc(high.sem, 1)
                if quant:
                    for u in range(2):
                        c = it * 2 + u
                        act.wait_ge(scored.sem, scored.done(c))
                        act.wait_ge(kept.sem, kept.free(c))
                        act.activation(o16[:, u], psl[u][:], ACT.Copy).then_inc(rounded.sem, 1)

        @block.tensor
        def _(pe):
            for s in (returned, turned, scored):
                pe.nop().then_inc(s.sem, s.credit)
            if add_y:
                with pe.Fori(0, PAIRS) as it:
                    for u in range(2):
                        c = it * 2 + u
                        pe.wait_ge(staged.sem, staged.done(c))
                        pe.wait_ge(added.sem, added.free(c))
                        for t in range(TPC):
                            last = pe.transpose(psa[u][:, D * t:D * t + D], ystage[:, u, D * t:D * t + D], k.ident[:])
                        last.then_inc(returned.sem, 1)
            if n_loads:
                pe.wait_ge(loaded.sem, loaded.done(n_loads - 1))
            if quant:
                pe.wait_ge(wquant.sem, wquant.done(0))
            with pe.Fori(0, PAIRS // 2) as i2:
                for w in range(2):
                    for u in range(2):
                        c = i2 * 4 + (2 * w + u)
                        pe.wait_ge(normed.sem, normed.done(c))
                        pe.wait_ge((taken if quant else high).sem, (taken if quant else high).free(c))
                        for t in range(TPC):
                            last = pe.transpose(psb[u][:, D * t:D * t + D], xn[:, 2 * w + u, t], k.ident[:])
                        last.then_inc(turned.sem, 1)
                    for u in range(2):
                        c = i2 * 4 + (2 * w + u)
                        if router:
                            pe.wait_ge(taken.sem, taken.done(c))
                            pe.wait_ge(kept.sem, kept.free(c))
                            for t in range(TPC):
                                last = pe.matmul(psl[u][:, E * t:E * t + E], xs[:, u, D * t:D * t + D], wr[:],
                                                 start=True, stop=True, skip_group_check=True)
                            last.then_inc(scored.sem, 1)
                        if quant:
                            pe.wait_ge(low.sem, low.done(c))
                            pe.wait_ge(rounded.sem, rounded.free(c))
                            pe.matmul(psl[u][:], wq[:], x16[:, u], start=True, stop=True).then_inc(scored.sem, 1)

        if new_select:
            @block.gpsimd
            def _(pool):
                make_select(k, pool)
                if weights:
                    weights.split_first(pool)

        if add_xn:
            @block.gpsimd
            def _(pool):
                pool.nop().then_inc(xn_added.sem, xn_added.credit)
                with pool.Fori(0, PAIRS // 2) as it:
                    for u in range(4):
                        c = it * 4 + u
                        pool.wait_ge(normed.sem, normed.done(c))
                        pool.tensor_tensor(k.X[:, cols(c)], k.X[:, cols(c)],
                                                        xn[:, u].rearrange("p t d -> p (t d)"), ALU.add) \
                                                            .then_inc(xn_added.sem, 1)

        @block.vector
        def _(dve):
            for s in (added, stats, merged, kept_mv, var_eps, inverted, normed, low, kept, wquant) + \
                    ((high,) if quant else ()):
                dve.nop().then_inc(s.sem, s.credit)
            if n_loads:
                dve.wait_ge(loaded.sem, loaded.done(n_loads - 1))
            if quant:
                link(dve, dve.tensor_scalar(wf[:], wf[:], 448.0, -448.0, ALU.min, ALU.max))
                link(dve, dve.tensor_scalar(step[:].bitcast(U32), wf[:].bitcast(U32), 0x7F800000, None,
                                            ALU.bitwise_and))
                link(dve, dve.tensor_scalar(step[:], step[:], 2.0 ** -6, 1.5 * 2.0 ** 20, ALU.max, ALU.mult))
                link(dve, dve.tensor_tensor(wf[:], wf[:], step[:], ALU.add))
                dve.tensor_tensor(wq[:], wf[:], step[:], ALU.subtract).then_inc(wquant.sem, 1)
            with dve.Fori(0, PAIRS) as it:
                chunks = [(u, it * 2 + u) for u in range(2)]
                if add_y:
                    for u, c in chunks:
                        dve.wait_ge(returned.sem, returned.done(c))
                        dve.tensor_tensor(k.X[:, cols(c)], k.X[:, cols(c)], psa[u][:], ALU.add).then_inc(added.sem, 1)
                for u, c in chunks:
                    if add_y:
                        dve.wait_ge(added.sem, added.done(c))
                    dve.wait_ge(merged.sem, merged.free(c))
                    dve.sem_inc(k.passed, 1)
                    for t in range(TPC):
                        last = dve.bn_stats(bst[:, u, t], k.X[:, bass.ds(c * CH + D * t, D)])
                    last.then_inc(stats.sem, 1)
                for u, c in chunks:
                    dve.wait_ge(stats.sem, stats.done(c))
                    dve.wait_ge(kept_mv.sem, kept_mv.free(c))
                    dve.sem_inc(k.passed, 1)
                    for t in range(TPC):
                        last = dve.bn_aggr(agg[:, u, t], bst[:, u, t])
                    last.then_inc(merged.sem, 1)
                for u, c in chunks:
                    dve.wait_ge(merged.sem, merged.done(c))
                    dve.tensor_copy(mv[:, cols(c, TPC * 2)], agg[:, u].rearrange("p t s -> p (t s)")) \
                        .then_inc(kept_mv.sem, 1)
            dve.wait_ge(kept_mv.sem, kept_mv.done(CHUNKS - 1))
            dve.tensor_scalar(var[:], mv[:].rearrange("p (t s) -> p t s", s=2)[:, :, 1], EPS, None,
                                          ALU.add).then_inc(var_eps.sem, 1)
            dve.wait_ge(rooted.sem, rooted.done(0))
            dve.reciprocal(rstd[:], std[:]).then_inc(inverted.sem, 1)
            dve.wait_ge(inverted.sem, inverted.done(0))

            def normalise(i, w):
                for u in range(2):
                    c = i * 4 + (2 * w + u)
                    dve.wait_ge(turned.sem, turned.free(c))
                    if add_xn:
                        dve.wait_ge(xn_added.sem, xn_added.free(c))
                    for t in range(TPC):
                        last = dve.tensor_scalar(xn[:, 2 * (w % 2) + u, t], k.X[:, bass.ds(c * CH + D * t, D)],
                                                 mv[:, bass.ds(c * (TPC * 2) + 2 * t, 1)],
                                                 rstd[:, bass.ds(c * TPC + t, 1)], ALU.subtract, ALU.mult)
                    last.then_inc(normed.sem, 1)

            def split(i, w):
                chunks = [(u, i * 4 + (2 * w + u)) for u in range(2)]
                for u, c in chunks:
                    dve.wait_ge(taken.sem, taken.done(c))
                    if quant:
                        dve.sem_inc(k.passed, 1)
                        dve.tensor_copy(x8[:, u], xs[:, u], saturate=False).then_inc(high.sem, 1)
                        dve.wait_ge(high.sem, high.done(c))
                        dve.wait_ge(scored.sem, scored.free(c))
                        dve.sem_inc(k.passed, 1)
                        dve.tensor_copy(x16[:, u], x8[:, u]).then_inc(low.sem, 1)
                    else:
                        dve.wait_ge(high.sem, high.done(c))
                        dve.tensor_tensor(k.xn[:, 1, cols(c)], xs[:, u], k.xn[:, 0, cols(c)].bitcast(F32),
                                                  ALU.subtract).then_inc(low.sem, 1)
                if quant:
                    for u, c in chunks:
                        dve.wait_ge(rounded.sem, rounded.done(c))
                        dve.tensor_scalar(k.Y[:, cols(c)], o16[:, u], bq[:], None, ALU.add).then_inc(kept.sem, 1)
                if router:
                    for u, c in chunks:
                        dve.wait_ge(scored.sem, scored.done(c))
                        out = logits[:, cols(c, TPC * E)]
                        if br_dram is None:
                            dve.tensor_copy(out, psl[u][:, :TPC * E]).then_inc(kept.sem, 1)
                        else:
                            dve.tensor_tensor(out.rearrange("p (t e) -> p t e", e=E),
                                                       psl[u][:, :TPC * E].rearrange("p (t e) -> p t e", e=E),
                                                       br[:].unsqueeze(1).to_broadcast([128, TPC, E]), ALU.add) \
                                                           .then_inc(kept.sem, 1)

            normalise(0, 0)
            with dve.Fori(0, PAIRS // 2 - 1) as i:
                for w in range(2):
                    normalise(i, w + 1)
                    split(i, w)
            normalise(PAIRS // 2 - 1, 1)
            split(PAIRS // 2 - 1, 0)
            split(PAIRS // 2 - 1, 1)


def finish_phase(k, out):
    nc = k.nc
    with ExitStack() as here:
        ystage = k.sb("end_ystage", [128, 2, CH], F32, here)
        psa = [k.ps(f"end_psa{u}", here) for u in range(2)]
        staged = k.counter("staged", CHUNKS)
        returned = k.counter("returned", CHUNKS)
        added = k.counter("added", CHUNKS)
        stored = k.counter("stored", CHUNKS, 16)
        block = here.enter_context(nc.Block())

        @block.scalar
        def _(act):
            act.nop().then_inc(staged.sem, staged.credit)
            with act.Fori(0, PAIRS) as it:
                for u in range(2):
                    c = it * 2 + u
                    act.wait_ge(returned.sem, returned.free(c))
                    act.sem_inc(k.passed, 1)
                    act.activation(ystage[:, u], k.Y[:, cols(c)], ACT.Copy).then_inc(staged.sem, 1)

        @block.tensor
        def _(pe):
            pe.nop().then_inc(returned.sem, returned.credit)
            with pe.Fori(0, PAIRS) as it:
                for u in range(2):
                    c = it * 2 + u
                    pe.wait_ge(staged.sem, staged.done(c))
                    pe.wait_ge(added.sem, added.free(c))
                    for t in range(TPC):
                        last = pe.transpose(psa[u][:, D * t:D * t + D], ystage[:, u, D * t:D * t + D], k.ident[:])
                    last.then_inc(returned.sem, 1)

        @block.vector
        def _(dve):
            dve.nop().then_inc(added.sem, added.credit)
            with dve.Fori(0, PAIRS) as it:
                for u in range(2):
                    c = it * 2 + u
                    dve.wait_ge(returned.sem, returned.done(c))
                    dve.tensor_tensor(k.X[:, cols(c)], k.X[:, cols(c)], psa[u][:], ALU.add).then_inc(added.sem, 1)

        @block.sync
        def _(sp):
            sp.nop().then_inc(stored.sem, stored.credit)
            with sp.Fori(0, PAIRS) as it:
                for u in range(2):
                    c = it * 2 + u
                    sp.wait_ge(added.sem, added.done(c))
                    sp.sem_inc(k.passed, 1)
                    sp.dma_start(out[:, cols(c)], k.X[:, cols(c)]).then_inc(stored.sem, 16)
            sp.wait_ge(stored.sem, stored.done(CHUNKS - 1))


def route_phase(k, name, E, top, logits, rule, shared=0, bias=None, cap=None, weights=None):
    nc = k.nc
    W = TILES * E
    with ExitStack() as here:
        work = k.sb(f"{name}_work", [128, W], F32, here)
        val = k.sb(f"{name}_val", [128, W], F32, here)
        eq = k.sb(f"{name}_eq", [128, W], F32, here)
        comb = k.sb(f"{name}_comb", [128, W], F32, here)
        picks = k.sb(f"{name}_picks", [128, top, W], F32, here)
        rev = k.sb(f"{name}_rev", [128, E], F32, here)
        red = k.sb(f"{name}_red", [128, TILES], F32, here)
        parts = k.sb(f"{name}_parts", [128, TILES, 3, EP], BF16, here)
        psc = [k.ps(f"{name}_psc{u}", here, (128, CH), BF16) for u in range(2)]
        br = k.sb(f"{name}_br", [128, E], F32, here) if bias is not None else None
        loaded = k.counter("loaded", 1, 16) if bias is not None else None
        curves = 2 if rule == "sigmoid" else 1
        shifted = k.counter("shifted", curves)
        curved = k.counter("curved", curves)
        split = k.counter("parts_split", 1)
        pturned = k.counter("parts_turned", CHUNKS)
        pkept = k.counter("parts_kept", CHUNKS)
        const = k.chain("constants")
        link = k.chain("dve_steps")
        ready = k.counter("rev_ready", 1)
        masks_ready = k.counter("masks_ready", int(cap is not None))
        counted = k.counter("counted", int(cap is not None))
        if cap is not None:
            before = k.sb(f"{name}_before", [128, 128], BF16, here)
            ones = k.sb(f"{name}_ones", [128, 128], BF16, here)
            bits = k.sb(f"{name}_bits", [128, top * W], BF16, here)
            total = [k.sb(f"{name}_total{i}", [128, top * W], F32, here) for i in range(3)]
            ps_in = k.ps(f"{name}_ps_in", here)
            ps_all = k.ps(f"{name}_ps_all", here)
        block = here.enter_context(nc.Block())

        def v3(ap):
            return ap.rearrange("p (t e) -> p t e", e=E)

        @block.sync
        def _(sp):
            if bias is not None:
                sp.nop().then_inc(loaded.sem, loaded.credit)
                sp.dma_start(br[:], bias.partition_broadcast(128)).then_inc(loaded.sem, 16)
                sp.wait_ge(loaded.sem, loaded.done(0))
            if weights:
                weights.fetch(sp)

        @block.gpsimd
        def _(pool):
            pool.nop().then_inc(ready.sem, ready.credit)
            for e in range(E):
                last = pool.memset(rev[:, e:e + 1], float(E - e))
            const(pool, last)
            if cap is not None:
                const(pool, pool.memset(ones[:], 1.0))
                const(pool, pool.affine_select(out=before[:], in_=ones[:], compare_op=ALU.is_gt, fill=0.0,
                                               base=0, pattern=[[1, 128]], channel_multiplier=-1))
            const(pool, pool.memset(parts[:], 0.0))
            if shared:
                const(pool, pool.memset(parts[:, :, 0, E:E + shared], 1.0))
            pool.nop().then_inc(ready.sem, 1)
            if weights:
                weights.split_first(pool)

        @block.scalar
        def _(act):
            act.nop().then_inc(curved.sem, curved.credit)
            if rule == "sigmoid":
                act.wait_ge(shifted.sem, shifted.done(0))
                act.activation(val[:], logits[:], ACT.Sigmoid)
                act.activation(work[:], eq[:], ACT.Sigmoid).then_inc(curved.sem, 1)
                act.wait_ge(shifted.sem, shifted.done(1))
                act.activation(comb[:], comb[:], ACT.Exp).then_inc(curved.sem, 1)
            else:
                act.wait_ge(shifted.sem, shifted.done(0))
                act.activation(val[:], eq[:], ACT.Exp).then_inc(curved.sem, 1)

        @block.tensor
        def _(pe):
            for s in (pturned, counted):
                pe.nop().then_inc(s.sem, s.credit)
            if cap is not None:
                pe.wait_ge(ready.sem, ready.done(0))
                pe.wait_ge(masks_ready.sem, masks_ready.done(0))
                pe.matmul(ps_in[:, :top * W], before[:], bits[:], start=True, stop=True)
                pe.matmul(ps_all[:, :top * W], ones[:], bits[:], start=True, stop=True).then_inc(counted.sem, 1)
            pe.wait_ge(split.sem, split.done(0))
            flat = parts[:].rearrange("p t s e -> p (t s e)")
            with pe.Fori(0, PAIRS) as it:
                for u in range(2):
                    c = it * 2 + u
                    pe.wait_ge(pkept.sem, pkept.free(c))
                    for t in range(TPC):
                        last = pe.transpose(psc[u][:3 * EP, D * t:D * t + D], flat[:, bass.ds(c * (TPC * 3 * EP) + t * 3 * EP, 3 * EP)],
                                            k.identb[:])
                    last.then_inc(pturned.sem, 1)

        @block.vector
        def _(dve):
            for s in (shifted, split, pkept, masks_ready):
                dve.nop().then_inc(s.sem, s.credit)
            if bias is not None:
                dve.wait_ge(loaded.sem, loaded.done(0))
            if rule == "sigmoid":
                dve.tensor_tensor(v3(eq[:]), v3(logits[:]),
                                              br[:].unsqueeze(1).to_broadcast([128, TILES, E]), ALU.add) \
                                                  .then_inc(shifted.sem, 1)
                dve.wait_ge(curved.sem, curved.done(0))
            else:
                link(dve, dve.tensor_reduce(red[:], v3(logits[:]), AX.X, ALU.max))
                dve.tensor_tensor(v3(eq[:]), v3(logits[:]), spread(red[:], E), ALU.subtract).then_inc(shifted.sem, 1)
                dve.wait_ge(curved.sem, curved.done(0))
                if rule == "softmax":
                    link(dve, dve.tensor_reduce(red[:], v3(val[:]), AX.X, ALU.add))
                    link(dve, dve.reciprocal(red[:], red[:]))
                    link(dve, dve.tensor_tensor(v3(val[:]), v3(val[:]), spread(red[:], E), ALU.mult))
                    link(dve, dve.tensor_copy(work[:], val[:]))
                else:
                    link(dve, dve.tensor_copy(work[:], logits[:]))
            dve.wait_ge(ready.sem, ready.done(0))
            for j in range(top):
                link(dve, dve.tensor_reduce(red[:], v3(work[:]), AX.X, ALU.max))
                link(dve, dve.tensor_tensor(v3(eq[:]), v3(work[:]), spread(red[:], E), ALU.is_equal))
                link(dve, dve.tensor_tensor(v3(eq[:]), v3(eq[:]), rev[:].unsqueeze(1).to_broadcast([128, TILES, E]),
                                            ALU.mult))
                link(dve, dve.tensor_reduce(red[:], v3(eq[:]), AX.X, ALU.max))
                link(dve, dve.tensor_tensor(v3(picks[:, j]), v3(eq[:]), spread(red[:], E), ALU.is_equal))
                if j + 1 < top:
                    link(dve, dve.scalar_tensor_tensor(work[:], picks[:, j], -BIG, work[:], ALU.mult, ALU.add))
            mask = eq
            link(dve, dve.tensor_tensor(mask[:], picks[:, 0], picks[:, 1], ALU.add))
            for j in range(2, top):
                link(dve, dve.tensor_tensor(mask[:], mask[:], picks[:, j], ALU.add))
            link(dve, dve.tensor_tensor(comb[:], val[:], mask[:], ALU.mult))
            if rule == "sigmoid":
                link(dve, dve.tensor_reduce(red[:], v3(comb[:]), AX.X, ALU.max))
                dve.tensor_tensor(v3(comb[:]), v3(comb[:]), spread(red[:], E), ALU.subtract).then_inc(shifted.sem, 1)
                dve.wait_ge(curved.sem, curved.done(1))
                link(dve, dve.tensor_tensor(comb[:], comb[:], mask[:], ALU.mult))
            link(dve, dve.tensor_reduce(red[:], v3(comb[:]), AX.X, ALU.add))
            link(dve, dve.tensor_scalar(red[:], red[:], 1e-12, None, ALU.max))
            link(dve, dve.reciprocal(red[:], red[:]))
            link(dve, dve.tensor_tensor(v3(comb[:]), v3(comb[:]), spread(red[:], E), ALU.mult))
            if cap is not None:
                dve.tensor_copy(bits[:], picks[:].rearrange("p j w -> p (j w)")).then_inc(masks_ready.sem, 1)
                dve.wait_ge(counted.sem, counted.done(0))
                link(dve, dve.tensor_copy(total[2][:], ps_all[:, :top * W]))
                link(dve, dve.tensor_copy(total[0][:], total[2][:]))
                src, dst, s = total[0], total[1], E
                while s < top * W:
                    link(dve, dve.tensor_copy(dst[:, :s], src[:, :s]))
                    link(dve, dve.tensor_tensor(dst[:, s:], src[:, s:], src[:, :top * W - s], ALU.add))
                    src, dst, s = dst, src, 2 * s
                link(dve, dve.tensor_tensor(src[:], src[:], total[2][:], ALU.subtract))
                link(dve, dve.tensor_tensor(src[:], src[:], ps_in[:, :top * W], ALU.add))
                link(dve, dve.tensor_scalar(src[:], src[:], float(cap), None, ALU.is_lt))
                link(dve, dve.tensor_tensor(src[:], src[:], picks[:].rearrange("p j w -> p (j w)"), ALU.mult))
                link(dve, dve.tensor_tensor(mask[:], src[:, :W], src[:, W:], ALU.add))
                link(dve, dve.tensor_tensor(comb[:], comb[:], mask[:], ALU.mult))
            for part in range(3):
                link(dve, dve.tensor_copy(parts[:, :, part, :E], v3(comb[:])))
                if part < 2:
                    link(dve, dve.tensor_tensor(v3(comb[:]), v3(comb[:]), parts[:, :, part, :E], ALU.subtract))
            dve.nop().then_inc(split.sem, 1)
            with dve.Fori(0, PAIRS) as it:
                for u in range(2):
                    c = it * 2 + u
                    dve.wait_ge(pturned.sem, pturned.done(c))
                    dve.tensor_copy(k.combT[:, cols(c)], psc[u][:3 * EP, :]).then_inc(pkept.sem, 1)


AHEAD = 2
STEPS = 2 * CHUNKS
ROUND = 4


def moe_phase(k, name, E, kind, weights, b1_dram=None, b2_dram=None):
    nc = k.nc
    glu = kind == "swiglu"
    FT = 1 if glu else 4
    W1 = 2 * D if glu else FT * D
    WC = W1 + FT * D
    Q = WC // 4
    HB = CH if glu else 2 * CH
    PER = 1 if glu else 2
    RH = ROUND if glu else 3 - 1
    func = {"relu": ACT.Relu, "gelu": ACT.Gelu, "swiglu": ACT.Silu}[kind]
    half = E // 2
    steps = E * CHUNKS
    with ExitStack() as here:
        raw, wh, wl, w_dram = weights.raw, weights.wh, weights.wl, weights.w_dram
        hf = k.sb(f"{name}_hf", [128, 2, HB], F32, here)
        gate = k.sb(f"{name}_gate", [128, 2, CH], F32, here) if glu else None
        hh = k.sb(f"{name}_hh", [128, RH, PER * HB], F32R, here)
        hl = k.sb(f"{name}_hl", [128, RH, PER * HB], F32R, here)
        share = k.sb(f"{name}_share", [128, 2, CH], F32, here)
        yt = k.sb(f"{name}_yt", [128, 2, CH], F32, here)
        psu = [k.ps(f"{name}_psu{u}", here, (128, 2 * CH)) for u in range(2)]
        psy = [k.ps(f"{name}_psy{u}", here) for u in range(2)]
        psc = [k.ps(f"{name}_psc{u}", here) for u in range(2)]
        if b1_dram is not None:
            b1 = k.sb(f"{name}_b1", [128, E * FT], F32, here)
            b2 = k.sb(f"{name}_b2", [128, E], F32, here)
        loaded = k.counter("loaded", 2 if b1_dram is not None else 0, 16)
        arrived = [k.counter(f"arrived{v}", half, 16) for v in range(2)]
        whigh = k.counter("w_high", 4 * E, slots=8)
        wsplit = k.counter("w_split", 4 * E, slots=8)
        first = k.counter("first_product", PER * steps)
        gated = k.counter("gated", steps if glu else 0)
        hidden = k.counter("hidden", PER * steps)
        hhigh = k.counter("h_high", PER * steps)
        hsplit = k.counter("h_split", PER * steps)
        second = k.counter("second_product", steps, slots=RH)
        bcast = k.counter("share_product", steps)
        shared = k.counter("share_kept", steps)
        weighed = k.counter("weighed", steps)
        summed = k.counter("summed", steps)
        cleared = k.counter("cleared", 1)
        block = here.enter_context(nc.Block())

        def sweep(eng, step):
            with eng.Fori(0, half - 1) as i:
                for j in range(STEPS):
                    step(i, j, False)
            for j in range(STEPS):
                step(half - 1, j, True)

        def ahead(i, j, last, n):
            if last and j + n >= STEPS:
                return None
            return i, j + n

        @block.sync
        def _(sp):
            sp.nop().then_inc(loaded.sem, loaded.credit)
            for a in arrived:
                sp.nop().then_inc(a.sem, a.credit)
            if b1_dram is not None:
                sp.dma_start(b1[:], b1_dram).then_inc(loaded.sem, 16)
                sp.dma_start(b2[:], b2_dram).then_inc(loaded.sem, 16)
            for v in range(2):
                sp.wait_ge(weights.fetched[v].sem, weights.fetched[v].done(0))
                sp.nop().then_inc(arrived[v].sem, 16)
            with sp.Fori(0, half - 1) as i:
                for v in range(2):
                    sp.wait_ge(wsplit.sem, wsplit.free(i * 8 + (4 * v + 11)))
                    sp.sem_inc(k.passed, 1)
                    sp.dma_start(raw[:, v], w_dram[:, bass.ds(i * (2 * WC) + (v + 2) * WC, WC)]) \
                        .then_inc(arrived[v].sem, 16)

        @block.gpsimd
        def _(pool):
            for s in (whigh, wsplit, summed):
                pool.nop().then_inc(s.sem, s.credit)

            def split(i, v, q):
                n = i * 8 + (4 * v + q)
                part = slice(q * Q, q * Q + Q)
                pool.tensor_scalar(wh[:, v % 2, part], raw[:, v % 2, part], 1.0, None, ALU.mult) \
                    .then_inc(whigh.sem, 1)
                pool.wait_ge(whigh.sem, whigh.done(n))
                pool.tensor_tensor(wl[:, v % 2, part], raw[:, v % 2, part],
                                              wh[:, v % 2, part].bitcast(F32), ALU.subtract).then_inc(wsplit.sem, 1)

            pool.wait_ge(weights.first_split.sem, weights.first_split.done(0))
            for q in range(4):
                pool.nop().then_inc(whigh.sem, 1)
                pool.nop().then_inc(wsplit.sem, 1)
            pool.wait_ge(cleared.sem, cleared.done(0))

            def step(i, j, last):
                c, v = j % CHUNKS, j // CHUNKS
                if 1 <= c <= 4 and not (last and v == 1):
                    if c == 1:
                        if v == 0:
                            pool.wait_ge(arrived[1].sem, arrived[1].done(i))
                        else:
                            pool.wait_ge(arrived[0].sem, arrived[0].done(i + 1))
                        pool.wait_ge(second.sem, second.free(i * STEPS + (j - c - 1 + RH)))
                        pool.sem_inc(k.passed, 1)
                    split(i, v + 1, c - 1)
                t = i * STEPS + j
                pool.wait_ge(weighed.sem, weighed.done(t))
                pool.wait_ge(summed.sem, summed.free(t))
                pool.tensor_tensor(k.Y[:, c * CH:c * CH + CH], k.Y[:, c * CH:c * CH + CH], yt[:, j % 2],
                                              ALU.add).then_inc(summed.sem, 1)

            sweep(pool, step)

        @block.tensor
        def _(pe):
            for s in (first, second, bcast):
                pe.nop().then_inc(s.sem, s.credit)

            def up(i, j):
                c, v = j % CHUNKS, (j // CHUNKS) % 2
                t = i * STEPS + j
                xh, xl = (k.xn[:, part, c * CH:c * CH + CH] for part in range(2))
                if c == 0:
                    pe.wait_ge(wsplit.sem, wsplit.done(i * 8 + (4 * (j // CHUNKS) + 3)))
                for p in range(PER):
                    if glu:
                        pe.wait_ge(hidden.sem, hidden.free(t))
                    else:
                        pe.wait_ge(hidden.sem, hidden.free(i * (PER * STEPS) + (PER * j + p)))
                    bank = psu[j % 2 if glu else p]
                    for f in range(2):
                        w = slice((2 * p + f) * D, (2 * p + f) * D + D)
                        last = mm3(pe, bank[:, f * CH:f * CH + CH], wh[:, v, w], wl[:, v, w], xh, xl)
                    last.then_inc(first.sem, 1)

            def down(i, j):
                c, v = j % CHUNKS, j // CHUNKS
                t = i * STEPS + j
                pe.wait_ge(shared.sem, shared.free(t))
                pe.matmul(psc[j % 2][:], k.select[:3 * EP, bass.ds(i * (2 * D) + v * D, D)],
                                    k.combT[:, c * CH:c * CH + CH], start=True, stop=True).then_inc(bcast.sem, 1)
                pe.wait_ge(weighed.sem, weighed.free(t))
                for p in range(PER):
                    pe.wait_ge(hsplit.sem, hsplit.done(i * (PER * STEPS) + (PER * j + p)))
                    for f in range(2 if PER == 2 else 1):
                        n = 2 * p + f
                        w = slice(W1 + n * D, W1 + n * D + D)
                        h = slice(n * CH, n * CH + CH)
                        last = mm3(pe, psy[j % 2][:], wh[:, v, w], wl[:, v, w], hh[:, j % RH, h], hl[:, j % RH, h],
                                   start=n == 0, stop=n == FT - 1)
                last.then_inc(second.sem, 1)

            ahead_of = AHEAD if glu else 1
            for j in range(ahead_of):
                up(0, j)

            def step(i, j, last):
                nxt = ahead(i, j, last, ahead_of)
                if nxt:
                    up(*nxt)
                down(i, j)

            sweep(pe, step)

        @block.scalar
        def _(act):
            for s in (shared, gated) + ((hhigh,) if glu else (hidden,)):
                act.nop().then_inc(s.sem, s.credit)
            if b1_dram is not None:
                act.wait_ge(loaded.sem, loaded.done(1))

            def front(i, j):
                t = i * STEPS + j
                if glu:
                    act.wait_ge(first.sem, first.done(t))
                    act.wait_ge(hidden.sem, hidden.free(t))
                    act.activation(gate[:, j % 2], psu[j % 2][:, :CH], func).then_inc(gated.sem, 1)
                    return
                for p in range(PER):
                    n = i * (PER * STEPS) + (PER * j + p)
                    act.wait_ge(first.sem, first.done(n))
                    act.wait_ge(hsplit.sem, hsplit.free(n))
                    act.sem_inc(k.passed, 1)
                    for f in range(2):
                        b = b1[:, bass.ds(i * (2 * FT) + (j // CHUNKS) * FT + 2 * p + f, 1)] if b1_dram is not None \
                            else 0.0
                        last = act.activation(hf[:, p, f * CH:f * CH + CH], psu[p][:, f * CH:f * CH + CH], func, bias=b)
                    last.then_inc(hidden.sem, 1)

            def high(i, j):
                t = i * STEPS + j
                act.wait_ge(hidden.sem, hidden.done(t))
                act.wait_ge(second.sem, second.free(t))
                act.activation(hh[:, j % RH], hf[:, j % 2], ACT.Copy).then_inc(hhigh.sem, 1)

            def spread_share(i, j):
                t = i * STEPS + j
                act.wait_ge(bcast.sem, bcast.done(t))
                act.wait_ge(weighed.sem, weighed.free(t))
                act.activation(share[:, j % 2], psc[j % 2][:], ACT.Copy).then_inc(shared.sem, 1)

            ahead_of = AHEAD if glu else 1
            for j in range(ahead_of):
                front(0, j)
                if glu and j == 0:
                    high(0, 0)

            def step(i, j, last):
                nxt = ahead(i, j, last, ahead_of)
                if nxt:
                    front(*nxt)
                if glu and ahead(i, j, last, 1):
                    high(i, j + 1)
                spread_share(i, j)

            sweep(act, step)

        @block.vector
        def _(dve):
            for s in (hsplit, weighed, cleared) + ((hidden,) if glu else (hhigh,)):
                dve.nop().then_inc(s.sem, s.credit)
            dve.memset(k.Y[:], 0.0).then_inc(cleared.sem, 1)
            if b1_dram is not None:
                dve.wait_ge(loaded.sem, loaded.done(1))

            def front(i, j):
                t = i * STEPS + j
                if glu:
                    dve.wait_ge(gated.sem, gated.done(t))
                    dve.wait_ge(hsplit.sem, hsplit.free(t))
                    dve.tensor_tensor(hf[:, j % 2], gate[:, j % 2], psu[j % 2][:, CH:], ALU.mult) \
                        .then_inc(hidden.sem, 1)
                    return
                for p in range(PER):
                    n = i * (PER * STEPS) + (PER * j + p)
                    part = slice(p * HB, p * HB + HB)
                    dve.wait_ge(hidden.sem, hidden.done(n))
                    dve.wait_ge(second.sem, second.free(t))
                    dve.tensor_copy(hh[:, j % RH, part], hf[:, p]).then_inc(hhigh.sem, 1)
                    dve.wait_ge(hhigh.sem, hhigh.done(n))
                    dve.tensor_tensor(hl[:, j % RH, part], hf[:, p], hh[:, j % RH, part].bitcast(F32),
                                                 ALU.subtract).then_inc(hsplit.sem, 1)

            def low(i, j):
                t = i * STEPS + j
                dve.wait_ge(hhigh.sem, hhigh.done(t))
                dve.tensor_tensor(hl[:, j % RH], hf[:, j % 2], hh[:, j % RH].bitcast(F32), ALU.subtract) \
                    .then_inc(hsplit.sem, 1)

            def weigh(i, j):
                t = i * STEPS + j
                dve.wait_ge(second.sem, second.done(t))
                dve.wait_ge(shared.sem, shared.done(t))
                dve.wait_ge(summed.sem, summed.free(t))
                if b1_dram is not None:
                    dve.scalar_tensor_tensor(yt[:, j % 2], psy[j % 2][:],
                                                         b2[:, bass.ds(i * 2 + j // CHUNKS, 1)], share[:, j % 2],
                                                         ALU.add, ALU.mult).then_inc(weighed.sem, 1)
                else:
                    dve.tensor_tensor(yt[:, j % 2], psy[j % 2][:], share[:, j % 2], ALU.mult).then_inc(weighed.sem, 1)

            ahead_of = AHEAD if glu else 1
            for j in range(ahead_of):
                front(0, j)
                if glu and j == 0:
                    low(0, 0)

            def step(i, j, last):
                nxt = ahead(i, j, last, ahead_of)
                if nxt:
                    front(*nxt)
                if glu and ahead(i, j, last, 1):
                    low(i, j + 1)
                weigh(i, j)

            sweep(dve, step)


def attention_phase(k, name, kind, w_q=None, w_k=None, w_v=None, w_o=None, b_q=None, b_k=None, b_v=None, b_o=None,
                    ctx_tok=None):
    nc = k.nc
    stable = kind == "stablemax"
    project = w_q is not None
    scale = float(np.float32(1.0) / np.float32(np.sqrt(np.float32(HD))))
    BPC = TPC
    BODY = 2 * BPC
    NB = GROUPS if stable else 2
    with ExitStack() as here:
        flat = k.sb(f"{name}_flat", [128, 2, CH], F32R, here) if project else None
        mov = k.sb(f"{name}_mov", [128, 2, CH], F32R, here) if project else None
        stat = k.sb(f"{name}_stat", [128, 2, GROUPS, CH], F32R, here)
        ring = k.sb(f"{name}_ring", [128, 2, GROUPS, 4, 2 * D], F32R, here)
        vx = k.sb(f"{name}_vx", [128, 2, BPC, HEADS * HD], F32, here)
        vpad = k.select[:].bitcast(F32).rearrange("p (o h w) -> p o h w", o=2, h=OCT)
        oraw = k.sb(f"{name}_oraw", [128, 2, 2 * D], F32, here)
        vtmp = k.sb(f"{name}_vtmp", [128, CH], F32, here)
        rot = k.sb(f"{name}_rot", [128, 2, CH], F32, here)
        rs = k.sb(f"{name}_rs", [128, 2, HEADS], F32, here)
        ost = k.sb(f"{name}_ost", [128, 2, D], F32, here)
        ot = k.sb(f"{name}_ot", [128, 2, D], F32, here)
        wo = k.sb(f"{name}_wo", [D, D], F32, here)
        prob = k.Y[:].rearrange("p (s g c) -> p s g c", s=2, g=GROUPS)
        expd = k.scratch[:].rearrange("p (g c) -> p g c", g=GROUPS)
        if project:
            wraw = k.Y[:, :3 * D]
            wh = k.sb(f"{name}_wh", [D, 3 * D], F32R, here)
            wl = k.sb(f"{name}_wl", [D, 3 * D], F32R, here)
        if stable:
            ptmp = k.scratch[:, 2 * CH:3 * CH]
            bias = k.sb(f"{name}_bias", [128, 3], F32, here)
            bo = k.scratch[:, 3 * CH:3 * CH + D]
        else:
            mx = k.sb(f"{name}_mx", [128, 2, 4], F32, here)
        pss = [k.ps(f"{name}_pss{g}", here) for g in range(NB)]
        pst = [] if stable else [k.ps(f"{name}_pst{g}", here) for g in range(2)]
        pso = [k.ps(f"{name}_pso{u}", here) for u in range(2)]
        psm = k.ps(f"{name}_psm", here)
        psr = k.ps(f"{name}_psr", here)

        n_loads = (5 if stable else 1) + (3 if project else 0)
        loaded = k.counter("loaded", n_loads, 16)
        masked = [k.counter(f"masked{s}", CHUNKS, 16 * 4 * PIECES, slots=1) for s in range(2)]
        stat_in = [k.counter(f"stat_in{u}", CHUNKS // 2, 16 * PIECES, slots=1) for u in range(2)]
        mov_out = k.counter("mov_out", CHUNKS, 16 * (1 if project else 2), slots=1)
        stat_out = k.counter("stat_out", CHUNKS, 16, slots=1)
        v_in = k.counter("v_in", CHUNKS * (not project), 16, slots=1)
        wh_done = k.counter("proj_w_high", int(project))
        wl_done = k.counter("proj_w_low", int(project))
        zeroed = k.counter("zeroed", 4)
        half_zeroed = k.counter("half_zeroed", 1)
        pieces = k.counter("piece_product", 4 * CHUNKS * project, slots=1)
        piece_out = k.counter("piece_taken", 4 * CHUNKS * project, slots=1)
        tmp_high = k.counter("piece_high", 2 * CHUNKS * project, slots=1)
        mov_ready = k.counter("mov_ready", CHUNKS * project, slots=1)
        stat_ready = k.counter("stat_ready", CHUNKS * project)
        v_taken = k.counter("v_taken", CHUNKS * (not project), slots=1)
        score = k.counter("score", GROUPS * TILES, slots=32)
        curve = k.counter("curve", GROUPS * TILES)
        shift = k.counter("shift", GROUPS * TILES)
        exped = k.counter("exped", GROUPS * TILES)
        tposed = k.counter("tposed", GROUPS * TILES * (not stable), slots=4)
        probs = k.counter("probs", GROUPS * TILES, slots=NB)
        values = k.counter("values", TILES, slots=8)
        padded = k.counter("padded", 2 * TILES, slots=16)
        octets = k.counter("octets", TILES, slots=1)
        rawtaken = k.counter("rawtaken", TILES)
        rawturned = k.counter("rawturned", TILES)
        inverse = k.counter("inverse", TILES)
        onorm = k.counter("onorm", TILES)
        oturned = k.counter("oturned", TILES)
        otaken = k.counter("otaken", TILES)
        oproj = k.counter("oproj", TILES)
        xadded = k.counter("xadded", TILES, slots=1)
        bo_added = k.counter("bo_added", int(stable))
        block = here.enter_context(nc.Block())

        def sweep(eng, chunk_piece, scores, item, after_first=None):
            for q in range(4):
                chunk_piece(0, 0, q)
            for g in range(GROUPS):
                scores(0, 0, g)
            if after_first:
                after_first()

            def body(i, first=False, last=False):
                for j in range(BODY):
                    if not (last and j >= BPC):
                        chunk_piece(i, 1 + j // BPC, j % BPC)
                    item(i, j, not (last and j == BODY - 1), not (first and j == 0))

            body(0, first=True)
            with eng.Fori(1, CHUNKS // 2 - 1) as i:
                body(i)
            body(CHUNKS // 2 - 1, last=True)

        def chunk(i, u):
            return i * 2 + u

        def batch(i, j):
            return i * BODY + j

        mov_rows, stat_rows = k.mov_rows, k.stat_rows
        by_head = mov_rows.rearrange("(g r i) c -> r i g c", r=4, i=HD)
        by_group = stat_rows.rearrange("(g x) c -> x g c", x=4 * HD)

        def group(i, j, g):
            return i * (BODY * GROUPS) + (j * GROUPS + g)

        @block.sync
        def _(sp):
            for s in [loaded, v_in, mov_out, stat_out] + stat_in + masked:
                sp.nop().then_inc(s.sem, s.credit)
            if project:
                for n, w in enumerate((w_q, w_k, w_v)):
                    sp.dma_start(wraw[:, n * D:n * D + D], w).then_inc(loaded.sem, 16)
            if stable:
                for n, b in enumerate((b_q, b_k, b_v)):
                    sp.dma_start(bias[:, n:n + 1], b).then_inc(loaded.sem, 16)
                sp.dma_start(bo, b_o.partition_broadcast(128)).then_inc(loaded.sem, 16)
            sp.dma_start(wo[:], w_o).then_inc(loaded.sem, 16)
            with sp.Fori(0, CHUNKS // 2) as i:
                for u in range(2):
                    c = chunk(i, u)
                    if project:
                        sp.wait_ge(mov_ready.sem, mov_ready.done(c))
                        sp.sem_inc(k.passed, 1)
                        sp.dma_start(mov_rows[:, cols(c, 2 * CH)], mov[:].rearrange("p s q -> p (s q)").bitcast(F32)) \
                            .then_inc(mov_out.sem, 16)
                        sp.wait_ge(stat_ready.sem, stat_ready.done(c))
                        sp.sem_inc(k.passed, 1)
                        sp.dma_start(stat_rows[:, cols(c, 2 * CH)], flat[:].rearrange("p s q -> p (s q)").bitcast(F32)) \
                            .then_inc(stat_out.sem, 16)
                    else:
                        for part in range(2):
                            sp.dma_start(mov_rows[:, bass.ds(c * (2 * CH) + part * CH, CH)]
                                         .rearrange("p (t q) -> p t q", q=D),
                                         k.context[:, cols(c, TPC), part, :].bitcast(F32)).then_inc(mov_out.sem, 16)
                        sp.dma_start(stat_rows[:, cols(c, 2 * CH)].rearrange("p (s q) -> p s q", s=2),
                                     k.xn[:, :, cols(c)].bitcast(F32)).then_inc(stat_out.sem, 16)
                        sp.wait_ge(v_taken.sem, v_taken.free(c))
                        sp.sem_inc(k.passed, 1)
                        sp.dma_start(vtmp[:], ctx_tok[:, cols(c)]).then_inc(v_in.sem, 16)
                    sp.wait_ge(mov_out.sem, mov_out.done(c))
                    sp.sem_inc(k.passed, 1)
                    for half in range(2):
                        if half == 0:
                            sp.wait_ge(zeroed.sem, zeroed.done(0))
                        else:
                            sp.wait_ge(half_zeroed.sem, half_zeroed.done(0))
                        sp.wait_ge(score.sem, score.free(i * (4 * 8) + ((2 * u + half) * 8 + 23)))
                        sp.sem_inc(k.passed, 1)
                        for piece, part in enumerate((0, 1, 0)):
                            for h in range(4):
                                row = 4 * HD * piece + HD * h
                                tok = bass.ds(c * (2 * CH) + part * CH + 2 * D * half, 2 * D)
                                sp.dma_start(ring[row:row + HD, half, :, h, :].bitcast(F32),
                                             by_head[h][:, :, tok]).then_inc(masked[half].sem, 16)
                        if half == 0:
                            sp.wait_ge(stat_out.sem, stat_out.done(c))
                            sp.sem_inc(k.passed, 1)
                            sp.wait_ge(score.sem, score.free(i * (2 * GROUPS * BPC) + (u * GROUPS * BPC + 15)))
                            sp.sem_inc(k.passed, 1)
                            for piece, part in enumerate((0, 0, 1)):
                                row = 4 * HD * piece
                                sp.dma_start(stat[row:row + 4 * HD, u].bitcast(F32),
                                             by_group[:, :, bass.ds(c * (2 * CH) + part * CH, CH)]) \
                                    .then_inc(stat_in[u].sem, 16)

        @block.gpsimd
        def _(pool):
            pool.nop().then_inc(zeroed.sem, zeroed.credit)
            pool.nop().then_inc(bo_added.sem, bo_added.credit)
            pool.nop().then_inc(padded.sem, padded.credit)
            pool.memset(ring[:, 0].rearrange("p g h q -> p (g h q)").bitcast(F32), 0.0).then_inc(zeroed.sem, 1)
            pool.wait_ge(zeroed.sem, zeroed.done(0))
            pool.memset(vpad.rearrange("p o h w -> p (o h w)"), 0.0).then_inc(zeroed.sem, 1)
            pool.wait_ge(zeroed.sem, zeroed.done(1))
            pool.memset(vpad[:, :, :, HD:HD + 1], 1.0).then_inc(zeroed.sem, 1)
            pool.wait_ge(zeroed.sem, zeroed.done(2))
            pool.memset(stat[4 * HD * PIECES:].rearrange("p s g q -> p (s g q)").bitcast(F32), 0.0) \
                .then_inc(zeroed.sem, 1)
            pool.wait_ge(zeroed.sem, zeroed.done(3))
            if stable:
                pool.wait_ge(loaded.sem, loaded.done(n_loads - 1))
                pool.tensor_tensor(k.X[:].rearrange("p (t d) -> p t d", d=D),
                                                k.X[:].rearrange("p (t d) -> p t d", d=D),
                                                bo.unsqueeze(1).to_broadcast([128, TILES, D]), ALU.add) \
                                                    .then_inc(bo_added.sem, 1)
            with pool.Fori(0, CHUNKS // 2) as i:
                for j in range(BODY):
                    u, b = j // BPC, j % BPC
                    if b == 0:
                        if project:
                            pool.wait_ge(piece_out.sem, piece_out.done(i * 8 + (4 * u + 3)))
                        else:
                            pool.wait_ge(v_taken.sem, v_taken.done(chunk(i, u)))
                    for o in range(2):
                        if o == 0:
                            pool.wait_ge(octets.sem, octets.free(i * BODY + j))
                        else:
                            pool.wait_ge(values.sem, values.free(i * BODY + (j + 7)))
                        pool.sem_inc(k.passed, 1)
                        pool.tensor_copy(vpad[:, o, :, 0:HD],
                                                    vx[:, u, b, o * OCT * HD:(o + 1) * OCT * HD]
                                                    .rearrange("p (h d) -> p h d", h=OCT)).then_inc(padded.sem, 1)

        order = (0, 1) if stable else (1, 0)

        @block.tensor
        def _(pe):
            for s in (pieces, score, tposed, octets, values, rawturned, oturned, oproj):
                pe.nop().then_inc(s.sem, s.credit)
            pe.wait_ge(loaded.sem, loaded.done(n_loads - 1))
            pe.wait_ge(zeroed.sem, zeroed.done(3))
            pe.wait_ge(half_zeroed.sem, half_zeroed.done(0))
            if project:
                pe.wait_ge(wl_done.sem, wl_done.done(0))

            def chunk_piece(i, u, q):
                if not project:
                    return
                c = chunk(i, u)
                n = i * 8 + (4 * u + q)
                pe.wait_ge(piece_out.sem, piece_out.free(n))
                if q == 3:
                    pe.wait_ge(piece_out.sem, piece_out.done(i * 8 + (4 * u + 2)))
                    for t in range(TPC):
                        last = pe.transpose(psm[:, D * t:D * t + D], vtmp[:, D * t:D * t + D], k.ident[:])
                    last.then_inc(pieces.sem, 1)
                    return
                w = order[q] if q < 2 else 2
                w = slice(w * D, w * D + D)
                if q < 2 and order[q] == 0:
                    xh, xl = (k.xn[:, part, cols(c)] for part in range(2))
                else:
                    xh, xl = (k.context[:, cols(c, TPC), part, :] for part in range(2))
                mm3(pe, psm[:], wh[:, w], wl[:, w], xh, xl).then_inc(pieces.sem, 1)

            def scores(i, j, g):
                u, b, half = (j // BPC) % 2, j % BPC, (j // 2) % 2
                if g == 0:
                    pe.wait_ge(stat_in[u].sem, stat_in[u].done(i + j // BODY))
                    pe.wait_ge(masked[half].sem, masked[half].done(i * 2 + j // BPC))
                pe.wait_ge((probs if stable else shift).sem, (probs if stable else shift).free(group(i, j, g)))
                a = slice(b * D, b * D + D)
                pe.matmul(pss[g % NB][:], stat[:, u, g, a], ring[:, half, g, :, D * (b % 2):D * (b % 2) + D],
                                    start=True, stop=True).then_inc(score.sem, 1)

            def tpose(i, j, g):
                n = group(i, j, g)
                pe.wait_ge(exped.sem, exped.done(n))
                pe.wait_ge(probs.sem, probs.free(n))
                for h in range(4):
                    last = pe.transpose(pst[g % 2][:, D * h:D * h + D], expd[:, g, D * h:D * h + D], k.ident[:])
                last.then_inc(tposed.sem, 1)

            def times_v(i, j, g):
                n = batch(i, j)
                if g % 2 == 0:
                    pe.wait_ge(padded.sem, padded.done(i * (2 * BODY) + (2 * j + g // 2)))
                if g == 0:
                    pe.wait_ge(rawtaken.sem, rawtaken.free(n))
                pe.wait_ge(probs.sem, probs.done(group(i, j, g)))
                for h in range(4 * g, 4 * g + 4):
                    o, r = h // OCT, h % OCT
                    window = vpad[:, o].rearrange("p h w -> p (h w)")[:, D * r:D * r + D]
                    last = pe.matmul(pso[j % 2][:, D * o:D * o + D], window,
                                     prob[:, j % 2, g, D * (h % 4):D * (h % 4) + D], start=r == 0, stop=r == OCT - 1)
                if g == 1:
                    last.then_inc(octets.sem, 1)
                if g == GROUPS - 1:
                    last.then_inc(values.sem, 1)

            def turn_raw(i, j):
                pe.wait_ge(rawtaken.sem, rawtaken.done(batch(i, j)))
                pe.wait_ge(xadded.sem, xadded.free(batch(i, j)))
                for o in range(2):
                    last = pe.transpose(psr[:, 2 * D + D * o:3 * D + D * o], oraw[:, j % 2, D * o:D * o + D], k.ident[:])
                last.then_inc(rawturned.sem, 1)

            def turn(i, j):
                pe.wait_ge(onorm.sem, onorm.done(batch(i, j)))
                pe.transpose(psr[:, :D], ost[:, j % 2], k.ident[:]).then_inc(oturned.sem, 1)

            def out(i, j):
                pe.wait_ge(otaken.sem, otaken.done(batch(i, j)))
                pe.matmul(psr[:, D:2 * D], ot[:, j % 2], wo[:], start=True, stop=True,
                                    skip_group_check=True).then_inc(oproj.sem, 1)

            def item(i, j, more, behind):
                for g in range(GROUPS):
                    if more:
                        scores(i, j + 1, g)
                    if not stable:
                        tpose(i, j, g)
                    if g == 1 and behind:
                        turn_raw(i, j - 1)
                    if g > 0:
                        times_v(i, j, g - 1)
                    if g == 3 and behind:
                        turn(i, j - 1)
                times_v(i, j, GROUPS - 1)
                if behind:
                    out(i, j - 1)
                if not more:
                    turn_raw(i, j)
                    turn(i, j)
                    out(i, j)

            sweep(pe, chunk_piece, scores, item)

        @block.scalar
        def _(act):
            for s in (exped, rawtaken, otaken) + ((curve,) if stable else (probs,)):
                act.nop().then_inc(s.sem, s.credit)
            if stable:
                nc.scalar.preload_act_table_set("natural_log_exp_and_others")
                act.wait_ge(loaded.sem, loaded.done(n_loads - 1))

            def chunk_piece(i, u, q):
                if q != 2 or not project:
                    return
                n = i * 8 + (4 * u + q)
                act.wait_ge(pieces.sem, pieces.done(n))
                act.wait_ge(piece_out.sem, piece_out.free(n))
                if stable:
                    act.activation(vtmp[:], psm[:], ACT.Identity, bias=bias[:, 2:3]).then_inc(piece_out.sem, 1)
                else:
                    act.activation(vtmp[:], psm[:], ACT.Copy).then_inc(piece_out.sem, 1)

            def scores(i, j, g):
                n = group(i, j, g)
                act.wait_ge(shift.sem, shift.done(n))
                if stable:
                    act.wait_ge(probs.sem, probs.free(i * (BODY * GROUPS) + (j * GROUPS + g + 2)))
                    act.activation(expd[:, g % 2], rot[:, g % 2], ACT.Ln, bias=1.0).then_inc(curve.sem, 1)
                    act.wait_ge(curve.sem, curve.done(n))
                    act.activation(expd[:, g % 2], expd[:, g % 2], ACT.Exp, scale=-1.0).then_inc(exped.sem, 1)
                else:
                    act.wait_ge(tposed.sem, tposed.free(n))
                    act.activation(expd[:, g], rot[:, g % 2], ACT.Exp, scale=scale).then_inc(exped.sem, 1)

            def take_raw(i, j):
                act.wait_ge(values.sem, values.done(batch(i, j)))
                act.wait_ge(rawturned.sem, rawturned.free(batch(i, j)))
                act.activation(oraw[:, j % 2], pso[j % 2][:, :2 * D], ACT.Copy).then_inc(rawtaken.sem, 1)

            def take(i, j):
                act.wait_ge(oturned.sem, oturned.done(batch(i, j)))
                act.wait_ge(oproj.sem, oproj.free(batch(i, j)))
                act.activation(ot[:, j % 2], psr[:, :D], ACT.Copy).then_inc(otaken.sem, 1)

            def item(i, j, more, behind):
                for g in range(GROUPS):
                    if g == 0 and behind:
                        take_raw(i, j - 1)
                    if not stable:
                        act.wait_ge(tposed.sem, tposed.done(group(i, j, g)))
                        act.wait_ge(values.sem, values.free(i * BODY + (j + 6)))
                        act.activation(prob[:, j % 2, g], pst[g % 2][:], ACT.Copy).then_inc(probs.sem, 1)
                    if g == 3 and behind:
                        take(i, j - 1)
                    if more:
                        scores(i, j + 1, g)
                if not more:
                    take_raw(i, j)
                    take(i, j)

            sweep(act, chunk_piece, scores, item)

        @block.vector
        def _(dve):
            for s in (wh_done, wl_done, piece_out, tmp_high, mov_ready, stat_ready, v_taken, shift, inverse,
                      onorm, xadded) + ((probs,) if stable else (curve,)):
                dve.nop().then_inc(s.sem, s.credit)
            dve.nop().then_inc(half_zeroed.sem, half_zeroed.credit)
            dve.memset(ring[:, 1].rearrange("p g h q -> p (g h q)").bitcast(F32), 0.0).then_inc(half_zeroed.sem, 1)
            dve.wait_ge(loaded.sem, loaded.done(n_loads - 1))
            if project:
                dve.tensor_copy(wh[:], wraw).then_inc(wh_done.sem, 1)
                dve.wait_ge(wh_done.sem, wh_done.done(0))
                dve.tensor_tensor(wl[:], wraw, wh[:].bitcast(F32), ALU.subtract).then_inc(wl_done.sem, 1)
                dve.wait_ge(wl_done.sem, wl_done.done(0))
            def chunk_piece(i, u, q):
                c = chunk(i, u)
                n = i * 8 + (4 * u + q)
                if q == 2:
                    return
                if q == 3:
                    dve.wait_ge(padded.sem, padded.free(i * (4 * BPC) + (2 * u * BPC + 7)))
                    if project:
                        dve.wait_ge(pieces.sem, pieces.done(n))
                        src = psm[:]
                    else:
                        dve.wait_ge(v_in.sem, v_in.done(c))
                        src = vtmp[:]
                    ins = dve.tensor_copy(vx[:, u % 2], src.rearrange("p (b d) -> p b d", b=BPC))
                    ins.then_inc((piece_out if project else v_taken).sem, 1)
                    return
                if not project:
                    return
                dve.wait_ge(pieces.sem, pieces.done(n))
                if q == 0:
                    dve.wait_ge(mov_out.sem, mov_out.free(c))
                    hi, lo, ready = mov[:, 0], mov[:, 1], mov_ready
                else:
                    dve.wait_ge(stat_out.sem, stat_out.free(c))
                    hi, lo, ready = flat[:, 0], flat[:, 1], stat_ready
                src = psm[:]
                if stable:
                    if q == 0:
                        dve.wait_ge(stat_ready.sem, stat_ready.free(i * 2 + (u + 1)))
                    else:
                        dve.wait_ge(mov_ready.sem, mov_ready.done(c))
                    dve.tensor_scalar(ptmp, psm[:], bias[:, q:q + 1], scale if q == 0 else 1.0,
                                                    ALU.add, ALU.mult).then_inc(piece_out.sem, 1)
                    dve.wait_ge(piece_out.sem, piece_out.done(n))
                    src = ptmp
                m = i * 4 + (2 * u + q)
                dve.tensor_copy(hi, src).then_inc(tmp_high.sem, 1)
                dve.wait_ge(tmp_high.sem, tmp_high.done(m))
                dve.tensor_tensor(lo, src, hi.bitcast(F32), ALU.subtract).then_inc(ready.sem, 1)
                if not stable:
                    dve.wait_ge(ready.sem, ready.done(c))
                    dve.nop().then_inc(piece_out.sem, 1)

            def front(i, j, g):
                n = group(i, j, g)
                dve.wait_ge(score.sem, score.done(n))
                if stable:
                    dve.wait_ge(curve.sem, curve.free(n))
                    dve.tensor_scalar(rot[:, g % 2], pss[g][:], -1.0, 0.0, ALU.mult, ALU.max).then_inc(shift.sem, 1)
                    return
                s3 = pss[g % 2][:].rearrange("p (h q) -> p h q", h=4)
                dve.wait_ge(shift.sem, shift.free(n))
                dve.tensor_reduce(mx[:, g % 2], s3, AX.X, ALU.max).then_inc(curve.sem, 1)
                dve.wait_ge(curve.sem, curve.done(n))
                dve.wait_ge(exped.sem, exped.free(n))
                dve.tensor_tensor(rot[:, g % 2].rearrange("p (h q) -> p h q", h=4), s3,
                                            spread(mx[:, g % 2], D), ALU.subtract).then_inc(shift.sem, 1)

            def back(i, j, g):
                dve.wait_ge(exped.sem, exped.done(group(i, j, g)))
                dve.wait_ge(values.sem, values.free(i * BODY + (j + 6)))
                dve.scalar_tensor_tensor(prob[:, j % 2, g], pss[g][:], 0.0, expd[:, g % 2],
                                                   ALU.max, ALU.add).then_inc(probs.sem, 1)

            def scores(i, j, g):
                front(i, j, g)
                if stable and g > 0:
                    back(i, j, g - 1)
                elif stable and j > 0:
                    back(i, j - 1, GROUPS - 1)

            def normalise(i, j):
                n = batch(i, j)
                dve.wait_ge(rawturned.sem, rawturned.done(n))
                o = psr[:, 2 * D:].rearrange("p (h v) -> p h v", v=HR)
                dve.wait_ge(onorm.sem, onorm.free(n))
                dve.reciprocal(rs[:, j % 2], o[:, :, HD]).then_inc(inverse.sem, 1)
                dve.wait_ge(inverse.sem, inverse.done(n))
                dve.wait_ge(oturned.sem, oturned.free(n))
                dve.tensor_tensor(ost[:, j % 2].rearrange("p (h d) -> p h d", d=HD), o[:, :, :HD],
                                            spread(rs[:, j % 2], HD), ALU.mult).then_inc(onorm.sem, 1)

            def add(i, j):
                n = batch(i, j)
                dve.wait_ge(oproj.sem, oproj.done(n))
                dve.tensor_tensor(k.X[:, cols(n, D)], k.X[:, cols(n, D)], psr[:, D:2 * D], ALU.add) \
                    .then_inc(xadded.sem, 1)

            def item(i, j, more, behind):
                if stable and not more:
                    back(i, j, GROUPS - 1)
                for g in range(GROUPS):
                    if more:
                        scores(i, j + 1, g)
                    if g == (1 if stable else 2) and behind:
                        normalise(i, j - 1)
                    if g == 3 and behind:
                        add(i, j - 1)
                if not more:
                    normalise(i, j)
                    add(i, j)

            def after_first():
                if stable:
                    dve.wait_ge(bo_added.sem, bo_added.done(0))

            sweep(dve, chunk_piece, scores, item, after_first)


def network(nc, a, out):
    with ExitStack() as ctx:
        k = Core(nc, ctx)
        k.X = k.sb("X", [128, N])
        k.Y = k.sb("Y", [128, N])
        k.xn = k.sb("xn", [128, 2, N], F32R)
        k.context = k.sb("context", [128, TILES, 2, D], F32R)
        k.scratch = k.sb("scratch", [128, N // 2])
        k.combT = k.scratch[:].bitcast(BF16)[:3 * EP, :]
        k.select = k.sb("select", [128, MAXE * D], BF16)
        k.ident = k.sb("ident", [D, D])
        k.identb = k.sb("identb", [D, D], BF16)

        k.mov_rows, k.stat_rows = (nc.dram_tensor(f"{s}_rows", (128, 2 * N), F32, kind="Internal").ap()
                                   for s in ("mov", "stat"))

        def logits(E):
            return k.scratch[:, :TILES * E]

        setup_phase(k, a["x"], a["ctxT"], a["L0x_Wg"], a["L0x_bg"], logits(8))
        route_phase(k, "r0", 8, 2, logits(8), "logits")
        with ExitStack() as here:
            w = Weights(k, "m0", "relu", a["L0x_w"], here)
            norm_phase(k, "n0", new_select=True, weights=w)
            moe_phase(k, "m0", 8, "relu", w, a["L0x_b1"], a["L0x_b2"])
        norm_phase(k, "n1", add_y=True, add_xn=True, router=(a["L0f_cT"], None, 8, logits(8)))
        with ExitStack() as here:
            w = Weights(k, "m1", "gelu", a["L0f_w"], here)
            route_phase(k, "r1", 8, 2, logits(8), "sigmoid", shared=2, bias=a["L0f_rb"], weights=w)
            moe_phase(k, "m1", 10, "gelu", w)
        norm_phase(k, "n2", add_y=True)
        attention_phase(k, "a1", "stablemax", *(a[f"L1x_W{w}"] for w in "qkvo"), *(a[f"L1x_b{w}"] for w in "qkvo"))
        norm_phase(k, "n3", router=(a["L1f_gT"], None, 8, logits(8)), new_select=True)
        with ExitStack() as here:
            w = Weights(k, "m3", "relu", a["L1f_w"], here)
            route_phase(k, "r3", 8, 2, logits(8), "softmax", cap=2 * N // 8, weights=w)
            moe_phase(k, "m3", 8, "relu", w, a["L1f_b1"], a["L1f_b2"])
        norm_phase(k, "n4", add_y=True)
        attention_phase(k, "a2", "softmax", w_o=a["L2x_Wo"], ctx_tok=a["ctx_tok"])
        norm_phase(k, "n5", quant=(a["L2f_wT"], a["L2f_b"]))
        norm_phase(k, "n6", add_y=True)
        attention_phase(k, "a3", "softmax", *(a[f"L3x_W{w}"] for w in "qkvo"))
        norm_phase(k, "n7", router=(a["L3f_rT"], a["L3f_rb"], 32, logits(32)), new_select=True)
        with ExitStack() as here:
            w = Weights(k, "m7", "swiglu", a["L3f_w"], here)
            route_phase(k, "r7", 32, 4, logits(32), "softmax", shared=4, weights=w)
            moe_phase(k, "m7", 36, "swiglu", w)
        finish_phase(k, out)


def _lay_out(v):
    v = {n: np.asarray(a) for n, a in v.items()}

    def tokens(x):
        return x.reshape(TILES, D, D).transpose(1, 0, 2).reshape(D, N)

    def first(w):
        return w.transpose(1, 0, 2)

    def second(w):
        e, f, d = w.shape
        return w.reshape(e, f // D, D, d).transpose(2, 0, 1, 3).reshape(D, e, f // D * d)

    def pack(*parts):
        return np.concatenate(parts, axis=2).reshape(D, -1)

    def bias1(b):
        return b.reshape(8, 4, D).transpose(2, 0, 1).reshape(D, 32)

    def heads(w):
        return w.transpose(1, 0, 2).reshape(D, D)

    def t(w):
        return w.swapaxes(-1, -2)

    def cut(w):
        return w.reshape(4, D, D)

    fc = np.concatenate([v["L0_ffn_Wfc_r"], v["L0_ffn_Wfc_sh"]])
    proj = np.concatenate([v["L0_ffn_Wproj_r"], v["L0_ffn_Wproj_sh"]])
    gate = np.concatenate([v["L3_ffn_gate_w"], cut(v["L3_ffn_sgate_w"])])
    up = np.concatenate([v["L3_ffn_up_w"], cut(v["L3_ffn_sup_w"])])
    down = np.concatenate([t(v["L3_ffn_down_w"]), cut(t(v["L3_ffn_sdown_w"]))])
    laid = {
        "x": tokens(v["x"]), "ctxT": v["ctx_1024"].reshape(N, D).T, "ctx_tok": tokens(v["ctx_1024"]),
        "L0x_Wg": v["L0_xattn_Wg"], "L0x_bg": v["L0_xattn_bg"],
        "L0x_w": pack(first(v["L0_xattn_W1"]), second(v["L0_xattn_W2"])),
        "L0x_b1": bias1(v["L0_xattn_b1"]), "L0x_b2": v["L0_xattn_b2"].T,
        "L0f_cT": v["L0_ffn_centroids"].T, "L0f_rb": v["L0_ffn_routing_bias"],
        "L0f_w": pack(first(t(fc)), second(t(proj))),
        **{f"L1x_W{w}": v[f"L1_xattn_W{w}"].T for w in "qkvo"},
        **{f"L1x_b{w}": v[f"L1_xattn_b{w}"].reshape(D, 1) for w in "qkv"}, "L1x_bo": v["L1_xattn_bo"],
        "L1f_gT": v["L1_ffn_gate_w"].T,
        "L1f_w": pack(first(t(v["L1_ffn_fc1_w"])), second(v["L1_ffn_fc2_w"])),
        "L1f_b1": bias1(v["L1_ffn_fc1_b"]), "L1f_b2": v["L1_ffn_fc2_b"].reshape(8, D).T,
        "L2x_Wo": v["L2_xattn_w_concat"].T, "L2f_wT": v["L2_ffn_weight"].T, "L2f_b": v["L2_ffn_bias"].reshape(D, 1),
        **{f"L3x_W{w}": heads(v[f"L3_xattn_W{w}"]) for w in "qkv"}, "L3x_Wo": v["L3_xattn_Wo"].T,
        "L3f_rT": v["L3_ffn_router_w"].T, "L3f_rb": v["L3_ffn_router_bias"],
        "L3f_w": pack(first(t(gate)), first(t(up)), second(down)),
    }
    return {f"in_{n}": np.ascontiguousarray(a) for n, a in laid.items()}


def kernel(**inputs):
    import concourse.bacc as bacc
    from concourse.bass_utils import run_bass_kernel_spmd

    nc = bacc.Bacc("TRN2", target_bir_lowering=False, num_devices=1)
    arrays = _lay_out(inputs)
    aps = {n[3:]: nc.dram_tensor(n, a.shape, mybir.dt.from_np(a.dtype), kind="ExternalInput").ap()
           for n, a in arrays.items()}
    out = nc.dram_tensor("out_x", (D, N), F32, kind="ExternalOutput").ap()
    network(nc, aps, out)
    result = run_bass_kernel_spmd(nc, [arrays], core_ids=[0])
    got = np.asarray(result.results[0]["out_x"])
    return np.ascontiguousarray(got.reshape(D, TILES, D).transpose(1, 0, 2))
```
